# Optimizing a Trainium2 kernel written in Bass

```python
import numpy as np
import jax
import jax.numpy as jnp

def _softmax(x, axis=-1):
    return jax.nn.softmax(x, axis=axis)

def _gelu(x):
    return jax.nn.gelu(x, approximate=True)

def _silu(x):
    return jax.nn.silu(x)

def _sigmoid(x):
    return jax.nn.sigmoid(x)

def _layernorm(x, axis=-1, eps=1e-05):
    m = jnp.mean(x, axis=axis, keepdims=True)
    v = jnp.var(x, axis=axis, keepdims=True)
    return (x - m) / jnp.sqrt(v + eps)

def _scatter_add(tgt, idx, src, axis=0):
    return tgt.at[idx].add(src)

def _segment_sum(src, seg, n):
    return jax.ops.segment_sum(src, seg, n)
kernel_name = 'mk_early_fusion_d1_tok_img256_r4_fecab6'

def setup_inputs(seed: int=0):
    np.random.seed(seed)
    _w = jnp.asarray

    def _rec_inputs():
        import jax
        import jax.numpy as jnp
        _rk = jax.random.key(seed)
        x = -0.0003702 + 0.999946 * jax.random.normal(jax.random.fold_in(_rk, 1), (64, 1, 64, 64), jnp.float32)
        txt = 0.281643 + 0.58738 * jax.random.normal(jax.random.fold_in(_rk, 2), (64, 128, 64), jnp.float32)
        return (x, txt)
    x, txt = _rec_inputs()

    def _L0_tok_setup():
        import jax, jax.numpy as jnp
        import numpy as np
        PH, PW = (64, 25)
        SH, SW = (64, 12)

        def _unfold(x, ph, pw, sh, sw):
            B, C, H, W = x.shape
            nh = (H - ph) // sh + 1
            nw = (W - pw) // sw + 1
            rows = jnp.arange(nh)[:, None] * sh + jnp.arange(ph)[None, :]
            cols = jnp.arange(nw)[:, None] * sw + jnp.arange(pw)[None, :]
            p = x[:, :, rows, :]
            p = p[:, :, :, :, cols]
            p = jnp.transpose(p, (0, 2, 4, 1, 3, 5))
            return p.reshape(B, nh * nw, C * ph * pw)
        key = jax.random.key(seed)
        kx, kw = jax.random.split(key, 2)
        x = jax.random.normal(kx, (64, 1, 64, 1000), dtype=jnp.float32)
        in_dim = 1 * PH * PW
        weight = jax.random.normal(kw, (in_dim, 64), dtype=jnp.float32) / np.sqrt(in_dim).astype(np.float32)
        bias = jnp.zeros((64,), dtype=jnp.float32)
        return {'x': x, 'weight': weight, 'bias': bias}
    _L0_tok_all = _L0_tok_setup()
    _L0_tok_in = {k: v for k, v in _L0_tok_all.items() if k in ('weight', 'bias')}
    del _L0_tok_all

    def _L0_attn_setup():
        import jax, jax.numpy as jnp
        import numpy as np
        B, T, C = (16, 512, 64)
        TT = T
        LAYER_ID, N_LAYER = (3, 6)
        key = jax.random.key(seed)
        ks = jax.random.split(key, 6)
        ratio_0_to_1 = LAYER_ID / (N_LAYER - 1)
        ratio_1_to_almost0 = 1.0 - LAYER_ID / N_LAYER
        h = np.arange(TT, dtype=np.float32)
        decay_speed = -5.0 + 8.0 * (h / (TT - 1)) ** (0.7 + 1.3 * ratio_0_to_1)
        curve = -(TT - 1 - h)
        time_w = jnp.asarray(np.exp(np.clip(curve * decay_speed, -30.0, 0.0)), dtype=jnp.float32)
        i = np.arange(C, dtype=np.float32) / C
        time_mix_k = jnp.asarray((i ** ratio_1_to_almost0).reshape(1, 1, C), dtype=jnp.float32)
        time_mix_v = jnp.asarray((i ** ratio_1_to_almost0 + 0.3 * ratio_0_to_1).reshape(1, 1, C), dtype=jnp.float32)
        time_mix_r = jnp.asarray((i ** (0.5 * ratio_1_to_almost0)).reshape(1, 1, C), dtype=jnp.float32)
        x = jax.random.normal(ks[0], (B, T, C), dtype=jnp.float32)
        scale = 0.02
        Wk = scale * jax.random.normal(ks[1], (C, C), dtype=jnp.float32)
        Wv = scale * jax.random.normal(ks[2], (C, C), dtype=jnp.float32)
        Wr = scale * jax.random.normal(ks[3], (C, C), dtype=jnp.float32)
        Wo = scale * jax.random.normal(ks[4], (C, C), dtype=jnp.float32)
        return {'x': x, 'time_w': time_w, 'time_mix_k': time_mix_k, 'time_mix_v': time_mix_v, 'time_mix_r': time_mix_r, 'Wk': Wk, 'Wv': Wv, 'Wr': Wr, 'Wo': Wo}
    _L0_attn_all = _L0_attn_setup()
    _L0_attn_in = {k: v for k, v in _L0_attn_all.items() if k in ('time_w', 'time_mix_k', 'time_mix_v', 'time_mix_r', 'Wk', 'Wv', 'Wr', 'Wo')}
    del _L0_attn_all

    def _L0_ffn_setup():
        import jax, jax.numpy as jnp
        import numpy as np
        DIM = 64
        HEADS = 8
        NUM_KEYS = 64
        NUM_KV = NUM_KEYS ** 2
        PK_TOPK = 16
        FINAL_TOPK = 16
        DIM_KEY = DIM // 2
        P = 2

        def _pk(x, Wq_pk, pk_keys):
            b, n, _ = x.shape
            q = (x @ Wq_pk).reshape(b, n, P, HEADS, DIM_KEY).transpose(2, 0, 1, 3, 4)
            sim = jnp.einsum('pbnhd,pkhd->pbnhk', q, pk_keys)
            scores, idx = jax.lax.top_k(sim, PK_TOPK)
            idx0 = idx[0]
            idx1 = idx[1] * NUM_KEYS
            index = (idx0[..., :, None] + idx1[..., None, :]).reshape(b, n, HEADS, PK_TOPK * PK_TOPK)
            score = (scores[0][..., :, None] + scores[1][..., None, :]).reshape(b, n, HEADS, PK_TOPK * PK_TOPK)
            final_scores, pk_idx = jax.lax.top_k(score, FINAL_TOPK)
            final_indices = jnp.take_along_axis(index, pk_idx, axis=-1)
            final_scores = jax.nn.softmax(final_scores, axis=-1)
            return (final_scores, final_indices)
        key = jax.random.key(seed)
        ks = jax.random.split(key, 7)
        b, n = (2, 256)
        std = 0.02
        x = jax.random.normal(ks[0], (b, n, DIM), dtype=jnp.float32)
        Wq_pk = jax.random.normal(ks[1], (DIM, P * HEADS * DIM_KEY), dtype=jnp.float32) * std
        pk_keys = jax.random.normal(ks[2], (P, NUM_KEYS, HEADS, DIM_KEY), dtype=jnp.float32) * std
        Wq = jax.random.normal(ks[3], (DIM, HEADS * DIM), dtype=jnp.float32) * std
        keys_table = jax.random.normal(ks[4], (NUM_KV * HEADS, DIM), dtype=jnp.float32) * std
        values_table = jax.random.normal(ks[5], (NUM_KV * HEADS, DIM), dtype=jnp.float32) * std
        Wo = jax.random.normal(ks[6], (DIM * HEADS, DIM), dtype=jnp.float32) * std
        return {'x': x, 'Wq_pk': Wq_pk, 'pk_keys': pk_keys, 'Wq': Wq, 'keys_table': keys_table, 'values_table': values_table, 'Wo': Wo}
    _L0_ffn_all = _L0_ffn_setup()
    _L0_ffn_in = {k: v for k, v in _L0_ffn_all.items() if k in ('Wq_pk', 'pk_keys', 'Wq', 'keys_table', 'values_table', 'Wo')}
    del _L0_ffn_all
    return {'x': x, 'txt': txt, 'L0_tok_weight': _L0_tok_in['weight'], 'L0_tok_bias': _L0_tok_in['bias'], 'L0_attn_time_w': _L0_attn_in['time_w'], 'L0_attn_time_mix_k': _L0_attn_in['time_mix_k'], 'L0_attn_time_mix_v': _L0_attn_in['time_mix_v'], 'L0_attn_time_mix_r': _L0_attn_in['time_mix_r'], 'L0_attn_Wk': _L0_attn_in['Wk'], 'L0_attn_Wv': _L0_attn_in['Wv'], 'L0_attn_Wr': _L0_attn_in['Wr'], 'L0_attn_Wo': _L0_attn_in['Wo'], 'L0_ffn_Wq_pk': _L0_ffn_in['Wq_pk'], 'L0_ffn_pk_keys': _L0_ffn_in['pk_keys'], 'L0_ffn_Wq': _L0_ffn_in['Wq'], 'L0_ffn_keys_table': _L0_ffn_in['keys_table'], 'L0_ffn_values_table': _L0_ffn_in['values_table'], 'L0_ffn_Wo': _L0_ffn_in['Wo']}

def reference(x, txt, L0_tok_weight, L0_tok_bias, L0_attn_time_w, L0_attn_time_mix_k, L0_attn_time_mix_v, L0_attn_time_mix_r, L0_attn_Wk, L0_attn_Wv, L0_attn_Wr, L0_attn_Wo, L0_ffn_Wq_pk, L0_ffn_pk_keys, L0_ffn_Wq, L0_ffn_keys_table, L0_ffn_values_table, L0_ffn_Wo):
    import jax
    import jax.numpy as jnp

    def _L0_tok_ref(x, weight, bias):
        import jax, jax.numpy as jnp
        import numpy as np
        PH, PW = (64, 25)
        SH, SW = (64, 12)

        def _unfold(x, ph, pw, sh, sw):
            B, C, H, W = x.shape
            nh = (H - ph) // sh + 1
            nw = (W - pw) // sw + 1
            rows = jnp.arange(nh)[:, None] * sh + jnp.arange(ph)[None, :]
            cols = jnp.arange(nw)[:, None] * sw + jnp.arange(pw)[None, :]
            p = x[:, :, rows, :]
            p = p[:, :, :, :, cols]
            p = jnp.transpose(p, (0, 2, 4, 1, 3, 5))
            return p.reshape(B, nh * nw, C * ph * pw)
        p = _unfold(x, PH, PW, SH, SW)
        return jax.nn.gelu(jnp.einsum('bnk,kd->bnd', p, weight) + bias, approximate=False)

    def _L0_attn_ref(x, time_w, time_mix_k, time_mix_v, time_mix_r, Wk, Wv, Wr, Wo):
        import jax, jax.numpy as jnp
        import numpy as np
        B, T, C = (16, 512, 64)
        TT = T
        LAYER_ID, N_LAYER = (3, 6)
        Bx, Tx, Cx = x.shape
        maxlen = time_w.shape[0]
        xx = jnp.pad(x, ((0, 0), (1, 0), (0, 0)))[:, :-1]
        xk = x * time_mix_k + xx * (1.0 - time_mix_k)
        xv = x * time_mix_v + xx * (1.0 - time_mix_v)
        xr = x * time_mix_r + xx * (1.0 - time_mix_r)
        k = jnp.exp(jnp.clip(xk @ Wk, -60.0, 30.0))
        v = xv @ Wv
        r = xr @ Wr
        sum_k = jnp.cumsum(k, axis=1)
        kv = k * v
        t_idx = jnp.arange(Tx)
        d = t_idx[:, None] - t_idx[None, :]
        W = jnp.where(d >= 0, time_w[jnp.clip(maxlen - 1 - d, 0, maxlen - 1)], 0.0)
        wkv = jnp.einsum('tu,buc->btc', W, kv)
        rwkv = jax.nn.sigmoid(r) * wkv / sum_k
        return rwkv @ Wo

    def _L0_ffn_ref(x, Wq_pk, pk_keys, Wq, keys_table, values_table, Wo):
        import jax, jax.numpy as jnp
        import numpy as np
        DIM = 64
        HEADS = 8
        NUM_KEYS = 64
        NUM_KV = NUM_KEYS ** 2
        PK_TOPK = 16
        FINAL_TOPK = 16
        DIM_KEY = DIM // 2
        P = 2

        def _pk(x, Wq_pk, pk_keys):
            b, n, _ = x.shape
            q = (x @ Wq_pk).reshape(b, n, P, HEADS, DIM_KEY).transpose(2, 0, 1, 3, 4)
            sim = jnp.einsum('pbnhd,pkhd->pbnhk', q, pk_keys)
            scores, idx = jax.lax.top_k(sim, PK_TOPK)
            idx0 = idx[0]
            idx1 = idx[1] * NUM_KEYS
            index = (idx0[..., :, None] + idx1[..., None, :]).reshape(b, n, HEADS, PK_TOPK * PK_TOPK)
            score = (scores[0][..., :, None] + scores[1][..., None, :]).reshape(b, n, HEADS, PK_TOPK * PK_TOPK)
            final_scores, pk_idx = jax.lax.top_k(score, FINAL_TOPK)
            final_indices = jnp.take_along_axis(index, pk_idx, axis=-1)
            final_scores = jax.nn.softmax(final_scores, axis=-1)
            return (final_scores, final_indices)
        b, n, d = x.shape
        q = (x @ Wq).reshape(b, n, HEADS, DIM) * DIM ** (-0.5)
        kv_scores, indices = _pk(x, Wq_pk, pk_keys)
        offsets = jnp.arange(HEADS, dtype=indices.dtype) * NUM_KV
        ind = indices + offsets[None, None, :, None]
        k = jnp.einsum('bnhk,bnhkd->bnhd', kv_scores, keys_table[ind])
        v = jnp.einsum('bnhk,bnhkd->bnhd', kv_scores, values_table[ind])
        sim = jnp.einsum('bihd,bjhd->bhij', q, k)
        neg = -jnp.finfo(sim.dtype).max
        causal = jnp.tril(jnp.ones((n, n), dtype=bool))
        sim = jnp.where(causal, sim, neg)
        attn = jax.nn.softmax(sim, axis=-1)
        out = jnp.einsum('bhij,bjhd->bhid', attn, v)
        out = out.transpose(0, 2, 1, 3).reshape(b, n, HEADS * DIM)
        return out @ Wo
    h = _L0_tok_ref(x, L0_tok_weight, L0_tok_bias)
    h = jnp.concatenate([h, txt], axis=1)
    h = h + _L0_attn_ref(_layernorm(h, axis=-1), L0_attn_time_w, L0_attn_time_mix_k, L0_attn_time_mix_v, L0_attn_time_mix_r, L0_attn_Wk, L0_attn_Wv, L0_attn_Wr, L0_attn_Wo)
    h = h + _L0_ffn_ref(_layernorm(h, axis=-1), L0_ffn_Wq_pk, L0_ffn_pk_keys, L0_ffn_Wq, L0_ffn_keys_table, L0_ffn_values_table, L0_ffn_Wo)
    return h

_drawn_inputs = setup_inputs


def setup_inputs(seed=0):
    import zlib

    import numpy as np

    out = dict(_drawn_inputs(seed))
    spreads = {'L0_tok_bias': (0.0, 0.457)}
    factors = {'L0_attn_time_w': 8.0,
     'L0_attn_time_mix_k': 8.0,
     'L0_attn_time_mix_v': 8.0,
     'L0_attn_time_mix_r': 8.0,
     'L0_attn_Wk': 8.0,
     'L0_attn_Wv': 8.0,
     'L0_attn_Wr': 8.0,
     'L0_attn_Wo': 8.0,
     'L0_ffn_Wq_pk': 64.0,
     'L0_ffn_pk_keys': 64.0,
     'L0_ffn_Wq': 64.0,
     'L0_ffn_keys_table': 64.0,
     'L0_ffn_values_table': 64.0,
     'L0_ffn_Wo': 64.0}
    for name, (base, spread) in spreads.items():
        noise = np.random.default_rng([zlib.crc32(name.encode()), seed]).standard_normal(out[name].shape)
        drawn = base * np.exp(spread * noise) if base else spread * noise
        out[name] = jnp.asarray(drawn.astype(out[name].dtype))
    for name, factor in factors.items():
        out[name] = (out[name] * factor).astype(out[name].dtype)
    return out
```

```python
import numpy as np
import concourse.bass as bass
from concourse import mybir
from contextlib import ExitStack

B, T, C = 64, 132, 64
NIMG, TXT = 4, 128
PH, PW, SW = 64, 25, 12
HALF = T // 2
N = B * T
HEADS, NK, TOP = 8, 64, 16
DK = 32
BLK, TILES = 384, 3
NBLK = N // BLK
NB = 3
ATT = NB * T
NPAD = NBLK * ATT
CHUNKS = NK * NK // 128
GRP = 4
STEPS = HEADS * NBLK
LAG = 3
EPS = 1e-5
LOWEST = -3.4028234663852886e38
FLOOR = -60000.0
CAND = [(0, 1, 16, 0), (1, 3, 8, 16), (4, 4, 4, 40), (8, 8, 1, 56)]
NCAND = 64


def hold(eng, semaphore, value, passed):
    eng.wait_ge(semaphore, value)
    eng.sem_inc(passed, 1)


def build(nc, x, txt, tok_w, tok_b, toeplitz, mix, wkvr, attn_wo, wqT, keysT, wq, table, wo, out):
    f32, f16, u32 = mybir.dt.float32, mybir.dt.float16, mybir.dt.uint32
    ALU, ACT, AX = mybir.AluOpType, mybir.ActivationFunctionType, mybir.AxisListType
    ctx = ExitStack()
    with ctx:
        def sb(name, shape, dt=f32):
            return ctx.enter_context(nc.sbuf_tensor(name, shape, dt))

        def sem(name):
            return ctx.enter_context(nc.semaphore(name))

        bank = [ctx.enter_context(nc.psum_tensor(f"bank{i}", [128, 512], f32)) for i in range(8)]

        h0_d = nc.dram_tensor("h0_d", (B * NIMG, C), f32, kind="Internal").ap()
        h1_d = nc.dram_tensor("h1_d", (N, C), f32, kind="Internal").ap()
        yT_d = nc.dram_tensor("yT_d", (C, NPAD), f32, kind="Internal").ap()
        m_d = nc.dram_tensor("m_d", (HEADS + 1, C, 2 * NK), f32, kind="Internal").ap()
        kv_d = nc.dram_tensor("kv_d", (HEADS + 1, 2 * C, NPAD), f32, kind="Internal").ap()
        o_d = nc.dram_tensor("o_d", (HEADS + 1, C, NPAD), f32, kind="Internal").ap()

        ident = sb("ident", [128, 128])
        ident16 = sb("ident16", [128, 128], f16)
        sel_mask = sb("sel_mask", [128, CHUNKS, 128], f16)
        sel_score = sb("sel_score", [128, 8, 128], f16)
        iota16 = sb("iota16", [128, NK], f16)
        causal = sb("causal", [HALF, 2, T])
        s_const = sem("s_const")
        passed = {e: sem("passed_" + e) for e in ("pe", "dve", "sp")}

        front(nc, ctx, sb, sem, bank, locals())
        main(nc, ctx, sb, sem, bank, locals())
        final(nc, ctx, sb, sem, bank, locals())


def front(nc, ctx, sb, sem, bank, env):
    f32, f16 = env["f32"], env["f16"]
    ALU, ACT, AX = env["ALU"], env["ACT"], env["AX"]
    x, txt, out = env["x"], env["txt"], env["out"]
    h0_d, h1_d, yT_d, m_d, kv_d = (env[k] for k in ("h0_d", "h1_d", "yT_d", "m_d", "kv_d"))
    ident, ident16, sel_mask, sel_score = (env[k] for k in ("ident", "ident16", "sel_mask", "sel_score"))
    iota16, causal, s_const = env["iota16"], env["causal"], env["s_const"]
    passed = env["passed"]
    with ExitStack() as local:
        def sb(name, shape, dt=f32):
            return local.enter_context(nc.sbuf_tensor(name, shape, dt))

        img = sb("img", [PH, B, C])
        patch_w = sb("patch_w", [PH, PW, C])
        patch_b = sb("patch_b", [C, 1])
        h0T = sb("h0T", [C, B * NIMG])
        h0 = sb("h0", [128, 2, C])
        wmix = sb("wmix", [128, 3, C])
        mixc = sb("mixc", [128, 3])
        wo1 = sb("wo1", [C, C])
        wT = sb("wT", [HALF, 2, T])
        tri = sb("tri", [HALF, 2, T])
        wqT_s = sb("wqT_s", [DK, 2 * HEADS, C])
        keysT_s = sb("keysT_s", [DK, 2 * HEADS, NK])
        m_s = sb("m_s", [C, 2 * HEADS * NK])
        zeros = sb("zeros", [128, NPAD])
        X = sb("X", [HALF, 2, GRP, C])
        XC = sb("XC", [HALF, 2 * GRP, C])
        SQ = sb("SQ", [HALF, 2 * GRP, C])
        Y = sb("Y", [HALF, 2, GRP, 2, C])
        stat = sb("stat", [HALF, 4, 2 * GRP])
        XT = sb("XT", [128, GRP, T + 1])
        KC = sb("KC", [HALF, 2, GRP, C])
        K = sb("K", [HALF, 2, GRP, C])
        KV = sb("KV", [HALF, 2, GRP, C])
        ER = sb("ER", [HALF, 2, GRP, C])
        DEN = sb("DEN", [HALF, 2 * GRP, C])
        RW = sb("RW", [HALF, 2, GRP, C])
        RWT = sb("RWT", [C, GRP, T])
        H1 = sb("H1", [HALF, 2, GRP, C])
        YT = sb("YT", [C, GRP, T])

        s_img = sem("s_img")
        s_wload = sem("s_wload")
        s_mload = sem("s_mload")
        s_patch, s_gelu, s_h0T, s_h0, s_h0_st = (sem(n) for n in ("s_patch", "s_gelu", "s_h0T", "s_h0", "s_h0_st"))
        s_wready, s_m, s_m_sb, s_m_st, s_zero, s_zero_st = (sem(n) for n in ("s_wready", "s_m", "s_m_sb", "s_m_st", "s_zero", "s_zero_st"))
        s_xin = sem("s_xin")
        s_cen = [sem(f"s_cen{i}") for i in range(2)]
        s_sq = [sem(f"s_sq{i}") for i in range(2)]
        s_var = [sem(f"s_var{i}") for i in range(2)]
        s_std = [sem(f"s_std{i}") for i in range(2)]
        s_norm = [sem(f"s_norm{i}") for i in range(2)]
        s_turn = [sem(f"s_turn{i}") for i in range(2)]
        s_xt, s_proj, s_clip, s_exp, s_kv, s_mix, s_rw, s_rwt, s_rwt_sb, s_ao, s_h1, s_h1_st, s_yt, s_yt_st = (
            sem(n) for n in ("s_xt", "s_proj", "s_clip", "s_exp", "s_kv", "s_mix", "s_rw", "s_rwt",
                             "s_rwt_sb", "s_ao", "s_h1", "s_h1_st", "s_yt", "s_yt_st"))

        groups = B // GRP
        def turned(rows, k):
            return bank[k][rows, 0:2 * T].rearrange("p (b t) -> p b t", b=2)

        block = local.enter_context(nc.Block())

        @block.sync
        def _(sp):
            with nc.allow_non_contiguous_dma(reason="rows of 256 bytes"):
                sp.dma_start(img[:], x.rearrange("b c h w -> h (b c) w")).then_inc(s_img, 16)
                sp.dma_start(patch_w[:], env["tok_w"].rearrange("(h w) d -> h w d", h=PH)).then_inc(s_img, 16)
                sp.dma_start(patch_b[:], env["tok_b"].rearrange("(d o) -> d o", o=1)).then_inc(s_img, 16)
                sp.dma_start(wmix[:].rearrange("p a b -> p (a b)"), env["wkvr"]).then_inc(s_wload, 16)
                sp.dma_start(mixc[:], env["mix"]).then_inc(s_wload, 16)
                sp.dma_start(wo1[:], env["attn_wo"]).then_inc(s_wload, 16)
                sp.dma_start(wT[:], env["toeplitz"].rearrange("(a u) t -> u a t", a=2)).then_inc(s_wload, 16)
                sp.dma_start(wqT_s[:], env["wqT"]).then_inc(s_mload, 16)
                sp.dma_start(keysT_s[:], env["keysT"]).then_inc(s_mload, 16)
                sp.wait_ge(s_zero, 1)
                sp.dma_start(kv_d[0], zeros[:]).then_inc(s_zero_st, 16)
                for h in range(1, HEADS + 1):
                    sp.dma_start(kv_d[h][:, N:NPAD], zeros[:, 0:NPAD - N]).then_inc(s_zero_st, 16)
                sp.dma_start(yT_d[:, N:NPAD], zeros[0:C, 0:NPAD - N]).then_inc(s_zero_st, 16)
                sp.wait_ge(s_m_sb, 1)
                for h in range(HEADS + 1):
                    sp.dma_start(m_d[h], m_s[:, 128 * (h % HEADS):128 * (h % HEADS) + 128]).then_inc(s_m_st, 16)
                sp.wait_ge(s_h0, 1)
                sp.dma_start(h0_d.rearrange("(k p) d -> p k d", k=2), h0[:]).then_inc(s_h0_st, 16)
                sp.wait_ge(s_h0_st, 16)
                h0_v = h0_d.rearrange("(b n) d -> n b d", n=NIMG)
                txt_v = txt.rearrange("b t d -> t b d")
                h1_v = h1_d.rearrange("(b a t) d -> t a b d", a=2, t=HALF)
                yT_v = yT_d[:, 0:N].rearrange("c (b t) -> c b t", t=T)
                with sp.Fori(0, groups) as g:
                    b = bass.ds(g * GRP, GRP)
                    sp.dma_start(X[0:NIMG, 0], h0_v[:, b, :]).then_inc(s_xin, 16)
                    sp.dma_start(X[NIMG:HALF, 0], txt_v[0:HALF - NIMG, b, :]).then_inc(s_xin, 16)
                    sp.dma_start(X[:, 1], txt_v[HALF - NIMG:TXT, b, :]).then_inc(s_xin, 16)
                    sp.wait_ge(s_h1, g + 1)
                    for a in range(2):
                        sp.dma_start(h1_v[:, a, b, :], H1[:, a]).then_inc(s_h1_st, 16)
                    sp.wait_ge(s_yt, g + 1)
                    sp.dma_start(yT_v[:, b, :], YT[:]).then_inc(s_yt_st, 16)
                    sp.wait_ge(s_h1_st, g * 32 + 32)
                    hold(sp, s_yt_st, g * 16 + 16, passed["sp"])
                sp.wait_ge(s_zero_st, 16 * (HEADS + 2))
                sp.wait_ge(s_m_st, 16 * (HEADS + 1))

        @block.gpsimd
        def _(pool):
            pool.memset(zeros[:], 0.0).then_inc(s_zero, 1)
            pool.memset(ident[:], 0.0)
            pool.memset(ident16[:], 0.0)
            pool.memset(tri[:], 1.0)
            pool.memset(sel_mask[:], 0.0)
            pool.memset(sel_score[:], 0.0)
            pool.memset(causal[:], 0.0)
            pool.iota(iota16[:], [[1, NK]], base=0, channel_multiplier=0, allow_small_or_imprecise_dtypes=True)
            pool.drain()

            def one_where_zero(tile, pattern, base):
                pool.affine_select(out=tile, in_=tile, compare_op=ALU.not_equal, fill=1.0, base=base,
                                   pattern=pattern, channel_multiplier=1)

            one_where_zero(ident[:], [[-1, 128]], 0)
            one_where_zero(ident16[:], [[-1, 128]], 0)
            pool.wait_ge(s_wload, 64)
            for a in range(2):
                for w in (tri, wT):
                    pool.affine_select(out=w[:, a, :], in_=w[:, a, :], compare_op=ALU.is_ge, fill=0.0,
                                       base=-HALF * a, pattern=[[1, T]], channel_multiplier=-1)
                pool.affine_select(out=causal[:, a, :], in_=causal[:, a, :], compare_op=ALU.is_ge, fill=LOWEST,
                                   base=HALF * a, pattern=[[-1, T]], channel_multiplier=1)
            sm = sel_mask[:].rearrange("r (q c) (a b) -> r q c a b", q=4, a=4)
            for q in range(4):
                one_where_zero(sm[:, q], [[-4, 8], [-1, 4], [0, 32]], -32 * (q // 2))
            ss = sel_score[:].rearrange("r c (a b) -> r c a b", a=4)
            pool.drain()
            for q in range(4):
                one_where_zero(sm[:, q], [[0, 8], [0, 4], [-1, 32]], -64 - 32 * (q % 2))
            for k in range(2):
                one_where_zero(ss, [[0, 8], [0, 4], [-1, 32]], -32 * k)
                pool.drain()
                one_where_zero(ss, [[-4, 8], [-1, 4], [0, 32]], -64 - 32 * k)
                pool.drain()
            pool.drain().then_inc(s_const, 1)

        @block.tensor
        def _(pe):
            pe.wait_ge(s_img, 48)
            for w in range(PW):
                last = nc.tensor.matmul(bank[0][0:C, 0:B * NIMG].rearrange("d (b n) -> d b n", n=NIMG),
                                        patch_w[:, w, :], img[:, :, w:w + SW * (NIMG - 1) + 1:SW],
                                        start=(w == 0), stop=(w == PW - 1))
            last.then_inc(s_patch, 1)
            pe.wait_ge(s_mload, 32)
            for k in range(2 * HEADS):
                last = nc.tensor.matmul(bank[2 + k // 8][0:C, (k % 8) * NK:(k % 8) * NK + NK],
                                        wqT_s[:, k, :], keysT_s[:, k, :], start=True, stop=True)
            last.then_inc(s_m, 1)
            pe.wait_ge(s_const, 1)
            pe.wait_ge(s_gelu, 1)
            for k in range(2):
                last = nc.tensor.transpose(bank[1][:, k * C:(k + 1) * C], h0T[:, k * 128:(k + 1) * 128], ident[0:C, 0:C])
            last.then_inc(s_h0T, 1)
            pe.wait_ge(s_wready, 1)
            pe.wait_ge(s_m_sb, 1)
            pe.wait_ge(s_h0, 1)
            with pe.Fori(0, groups) as g:
                v = g + 1
                hold(pe, s_norm[0], v, passed["pe"])
                for b in range(GRP):
                    for a in range(2):
                        last = nc.tensor.transpose(turned(slice(0, 128), b // 2)[:, b % 2, a * HALF:(a + 1) * HALF],
                                                   Y[:, a, b].rearrange("p d c -> p (d c)"), ident[0:HALF, 0:HALF])
                last.then_inc(s_turn[0], 1)
                pe.wait_ge(s_xt, v)
                for b in range(GRP):
                    for a in range(2):
                        last = nc.tensor.matmul(bank[2 + b][0:HALF, a * 192:a * 192 + 192],
                                                XT[:, b, a * HALF:(a + 1) * HALF], wmix[:].rearrange("p a b -> p (a b)"),
                                                start=True, stop=True)
                last.then_inc(s_proj, 1)
                pe.wait_ge(s_kv, v)
                for w, src, bk in ((wT, KV, 6), (tri, K, 7)):
                    dst = bank[bk][0:HALF, :]
                    rows = [src[:, u].rearrange("p b c -> p (b c)") for u in range(2)]
                    nc.tensor.matmul(dst[:, 0:256], w[:, 0, 0:HALF], rows[0], start=True, stop=True)
                    nc.tensor.matmul(dst[:, 256:512], w[:, 0, HALF:T], rows[0], start=True, stop=False)
                    last = nc.tensor.matmul(dst[:, 256:512], w[:, 1, HALF:T], rows[1], start=False, stop=True)
                last.then_inc(s_mix, 1)
                hold(pe, s_rw, v, passed["pe"])
                for b in range(GRP):
                    for a in range(2):
                        last = nc.tensor.transpose(turned(slice(0, C), b // 2)[:, b % 2, a * HALF:(a + 1) * HALF],
                                                   RW[:, a, b], ident[0:HALF, 0:HALF])
                last.then_inc(s_rwt, 1)
                hold(pe, s_rwt_sb, v, passed["pe"])
                for b in range(GRP):
                    for a in range(2):
                        k = a * GRP + b
                        last = nc.tensor.matmul(bank[2][0:HALF, k * C:(k + 1) * C], RWT[:, b, a * HALF:(a + 1) * HALF],
                                                wo1[:], start=True, stop=True)
                last.then_inc(s_ao, 1)
                hold(pe, s_norm[1], v, passed["pe"])
                for b in range(GRP):
                    for a in range(2):
                        last = nc.tensor.transpose(turned(slice(0, C), b // 2)[:, b % 2, a * HALF:(a + 1) * HALF],
                                                   Y[:, a, b, 0], ident[0:HALF, 0:HALF])
                last.then_inc(s_turn[1], 1)

        @block.scalar
        def _(act):
            act.wait_ge(s_patch, 1)
            nc.scalar.activation(h0T[:], bank[0][0:C, 0:B * NIMG], ACT.Gelu, bias=patch_b[:, 0:1]).then_inc(s_gelu, 1)
            act.wait_ge(s_m, 1)
            nc.scalar.activation(m_s[:, 0:512], bank[2][0:C, :], ACT.Copy)
            nc.scalar.activation(m_s[:, 512:1024], bank[3][0:C, :], ACT.Copy).then_inc(s_m_sb, 1)
            act.wait_ge(s_h0T, 1)
            nc.scalar.activation(h0[:].rearrange("p k c -> p (k c)"), bank[1][:, 0:128], ACT.Copy).then_inc(s_h0, 1)
            act.wait_ge(s_wready, 1)
            with act.Fori(0, groups) as g:
                v = g + 1
                for n in range(2):
                    act.wait_ge(s_cen[n], v)
                    nc.scalar.activation(SQ[:], XC[:], ACT.Square).then_inc(s_sq[n], 1)
                    act.wait_ge(s_var[n], v)
                    nc.scalar.activation(stat[:, 2], stat[:, 1], ACT.Sqrt).then_inc(s_std[n], 1)
                    act.wait_ge(s_turn[n], v)
                    if n == 1:
                        for k in range(2):
                            last = nc.scalar.activation(YT[:, 2 * k:2 * k + 2, :], turned(slice(0, C), k), ACT.Copy)
                        last.then_inc(s_yt, 1)
                        break
                    for k in range(2):
                        nc.scalar.activation(XT[0:C, 2 * k:2 * k + 2, 0:T], turned(slice(0, C), k), ACT.Copy)
                        last = nc.scalar.activation(XT[C:128, 2 * k:2 * k + 2, 1:T + 1], turned(slice(C, 128), k), ACT.Copy)
                    last.then_inc(s_xt, 1)
                    act.wait_ge(s_clip, v)
                    nc.scalar.activation(K[:], KC[:], ACT.Exp)
                    for b in range(GRP):
                        last = nc.scalar.activation(ER[:, :, b, :], bank[2 + b][0:HALF, 0:384].rearrange("p (a c) -> p a c", a=2)[:, :, 128:192],
                                                    ACT.Exp, scale=-1.0)
                    last.then_inc(s_exp, 1)
                    act.wait_ge(s_rwt, v)
                    for k in range(2):
                        last = nc.scalar.activation(RWT[:, 2 * k:2 * k + 2, :], turned(slice(0, C), k), ACT.Copy)
                    last.then_inc(s_rwt_sb, 1)

        @block.vector
        def _(dve):
            def norm(n, src, v):
                nc.vector.tensor_reduce(stat[:, 0], src, AX.X, ALU.add)
                dve.drain()
                nc.vector.tensor_scalar(stat[:, 3], stat[:, 0], 1.0 / C, None, ALU.mult)
                dve.drain()
                nc.vector.tensor_tensor(XC[:], src, stat[:, 3].unsqueeze(2).broadcast_to([HALF, 2 * GRP, C]),
                                        ALU.subtract).then_inc(s_cen[n], 1)
                dve.wait_ge(s_sq[n], v)
                nc.vector.tensor_reduce(stat[:, 0], SQ[:], AX.X, ALU.add)
                dve.drain()
                nc.vector.tensor_scalar(stat[:, 1], stat[:, 0], 1.0 / C, EPS, ALU.mult, ALU.add).then_inc(s_var[n], 1)
                dve.wait_ge(s_std[n], v)
                nc.vector.reciprocal(stat[:, 3], stat[:, 2])
                dve.drain()
                for d in range(2):
                    last = nc.vector.tensor_tensor(Y[:].rearrange("p a b d c -> p (a b) d c")[:, :, d, :], XC[:],
                                                   stat[:, 3].unsqueeze(2).broadcast_to([HALF, 2 * GRP, C]), ALU.mult)
                last.then_inc(s_norm[n], 1)

            nc.vector.memset(XT[C:128, :, 0:1], 0.0)
            dve.wait_ge(s_wload, 64)
            nc.vector.tensor_scalar(mixc[C:128, :], mixc[C:128, :], -1.0, 1.0, ALU.mult, ALU.add)
            dve.drain()
            for k in range(3):
                last = nc.vector.tensor_scalar(wmix[:, k, :], wmix[:, k, :], mixc[:, k:k + 1], None, ALU.mult)
            last.then_inc(s_wready, 1)
            with dve.Fori(0, groups) as g:
                v = g + 1
                dve.wait_ge(s_xin, g * 48 + 48)
                norm(0, X[:].rearrange("p a b c -> p (a b) c"), v)
                dve.wait_ge(s_proj, v)
                for b in range(GRP):
                    last = nc.vector.tensor_scalar(KC[:, :, b, :], bank[2 + b][0:HALF, 0:384].rearrange("p (a c) -> p a c", a=2)[:, :, 0:64],
                                                   -60.0, 30.0, ALU.max, ALU.min)
                last.then_inc(s_clip, 1)
                dve.wait_ge(s_exp, v)
                for b in range(GRP):
                    last = nc.vector.tensor_tensor(KV[:, :, b, :], bank[2 + b][0:HALF, 0:384].rearrange("p (a c) -> p a c", a=2)[:, :, 64:128],
                                                   K[:, :, b, :], ALU.mult)
                last.then_inc(s_kv, 1)
                dve.wait_ge(s_mix, v)
                er = ER[:].rearrange("p a b c -> p (a b c)")
                den = DEN[:].rearrange("p g c -> p (g c)")
                nc.vector.scalar_tensor_tensor(out=den, in0=er, scalar=1.0, in1=bank[7][0:HALF, :], op0=ALU.add, op1=ALU.mult)
                dve.drain()
                nc.vector.reciprocal(den, den)
                dve.drain()
                nc.vector.tensor_tensor(RW[:].rearrange("p a b c -> p (a b c)"), bank[6][0:HALF, :], den, ALU.mult).then_inc(s_rw, 1)
                dve.wait_ge(s_ao, v)
                nc.vector.tensor_tensor(H1[:].rearrange("p a b c -> p (a b c)"), bank[2][0:HALF, :],
                                        X[:].rearrange("p a b c -> p (a b c)"), ALU.add).then_inc(s_h1, 1)
                dve.wait_ge(s_h1, v)
                norm(1, H1[:].rearrange("p a b c -> p (a b) c"), v)


def main(nc, ctx, sb, sem, bank, env):
    f32, f16, u32 = env["f32"], env["f16"], env["u32"]
    ALU, ACT, AX = env["ALU"], env["ACT"], env["AX"]
    yT_d, m_d, kv_d, o_d = (env[k] for k in ("yT_d", "m_d", "kv_d", "o_d"))
    ident, ident16, sel_mask, sel_score = (env[k] for k in ("ident", "ident16", "sel_mask", "sel_score"))
    iota16, causal, s_const = env["iota16"], env["causal"], env["s_const"]
    table, wq = env["table"], env["wq"]
    passed = env["passed"]
    with ExitStack() as local:
        def sb(name, shape, dt=f32):
            return local.enter_context(nc.sbuf_tensor(name, shape, dt))

        tbl = sb("tbl", [128, CHUNKS, 2 * C])
        pairs = [sb(f"pairs{p}", [128, 2, 2, BLK], f16) for p in range(2)]
        ranks = [sb(f"ranks{p}", [128, BLK], f16) for p in range(2)]
        ex = [sb(f"ex{k}", [128, BLK]) for k in range(2)]
        wt = [sb(f"wt{k}", [128, BLK]) for k in range(4)]
        kv_s = sb("kv_s", [2 * C, BLK])
        yt = sb("yt", [C, BLK])
        mh = sb("mh", [C, 2 * NK])
        S = sb("S", [128, TILES, 2, NK])
        S2 = sb("S2", [128, TILES, 2, NK])
        val = sb("val", [128, TILES, 2, TOP])
        idx = sb("idx", [128, TILES, 2, TOP], u32)
        idxf = sb("idxf", [128, TILES, 2, TOP])
        cand = sb("cand", [128, TILES, NCAND])
        cand1 = sb("cand1", [128, TILES, NCAND])
        cand2 = sb("cand2", [128, TILES, NCAND])
        best = sb("best", [128, TILES, TOP])
        picked = sb("picked", [128, TILES, NCAND])
        kept = sb("kept", [128, TILES, TOP])
        junk = sb("junk", [128, TILES, TOP])
        norm = sb("norm", [128, 4, TILES])
        sc = sb("sc", [128, TILES, 2, NK])
        sc_hi = sb("sc_hi", [128, TILES, 2 * NK], f16)
        sc_lo = sb("sc_lo", [128, TILES, 2 * NK], f16)
        split = sb("split", [128, 2, BLK], f16)
        onehot = sb("onehot", [128, TILES, TOP, 2 * NK], f16)
        kT = sb("kT", [C, ATT])
        vT = sb("vT", [C, ATT])
        ya = sb("ya", [C, ATT])
        wqh = sb("wqh", [C, C])
        qT = sb("qT", [C, ATT])
        v_s = sb("v_s", [HALF, 2 * NB, C])
        sim = sb("sim", [HALF, 2 * NB, T])
        prob = sb("prob", [HALF, 2 * NB, T])
        probn = sb("probn", [HALF, 2 * NB, T])
        negmax = sb("negmax", [HALF, 2 * NB])
        psum_ = sb("psum_", [HALF, 2 * NB])
        prec = sb("prec", [HALF, 2 * NB])
        pT = sb("pT", [HALF, NB * 198])
        oT = sb("oT", [C, ATT])

        mask_b = [bank[0], bank[1]]
        score_b = [bank[2], bank[3]]
        kv_b = bank[4]
        A, Bk, Ck = bank[5], bank[6], bank[7]

        names = ["scores", "probs", "weights", "mixed", "kv_sb",
                 "sims", "sims_sb", "vals", "idxs", "idxf_sb", "cands", "best_v", "kept_n", "lnz", "shifted",
                 "hi", "lo", "turned", "split_sb", "ranks_ps", "ranks_sb", "oh_a",
                 "q_ps", "q_sb", "v_ps", "v_sb", "negmax", "att_exp", "att_rec", "att_p", "pt0", "pt0_sb",
                 "pt1", "pt1_sb", "pv", "o_sb"]
        s = {n: sem("m_" + n) for n in names}
        s_oh = [sem(f"m_oh{t}") for t in range(TILES)]
        s_sim = [sem(f"m_sim{b}") for b in range(NB)]
        s_msk = [sem(f"m_msk{b}") for b in range(NB)]
        d_tbl = [sem(f"d_tbl{k}") for k in range(4)]
        d_sel, d_kv, d_att, d_o = sem("d_sel"), sem("d_kv"), sem("d_att"), sem("d_o")
        d_pairs = [sem(f"d_pairs{p}") for p in range(2)]

        block = local.enter_context(nc.Block())

        def first(n):
            return isinstance(n, int) and n == 0

        @block.sync
        def _(sp):
            def load_table(h, k):
                sp.dma_start(tbl[:, 8 * k:8 * k + 8, :],
                             table[bass.ds(h, 1)].rearrange("o p c d -> (o p) c d")[:, 8 * k:8 * k + 8, :]).then_inc(d_tbl[k], 16)

            def load_selection(n):
                h, blk = n // NBLK, n % NBLK
                sp.dma_start(yt[:], yT_d[:, bass.ds(blk * BLK, BLK)]).then_inc(d_sel, 16)
                sp.dma_start(mh[:], m_d[bass.ds(h, 1)].rearrange("o c k -> (o c) k")).then_inc(d_sel, 16)

            def move_pairs(n, p):
                sp.wait_ge(s["split_sb"], n + 1)
                with nc.allow_non_contiguous_dma(reason="rows of 768 bytes"):
                    for x in range(2):
                        for k in range(2):
                            src = split[64 + 32 * k:96 + 32 * k, x, :]
                            sp.dma_start(pairs[p][32 * x:32 * x + 32, :, k, :],
                                         src.unsqueeze(1).broadcast_to([32, 2, BLK])).then_inc(d_pairs[p], 16)
                            src = split[32 * k:32 * k + 32, x, :]
                            sp.dma_start(pairs[p][64 + 32 * x:96 + 32 * x, k, :, :],
                                         src.unsqueeze(1).broadcast_to([32, 2, BLK])).then_inc(d_pairs[p], 16)

            def load_attention(n):
                m = n - LAG + NBLK
                h, t = m // NBLK, m % NBLK
                col = bass.ds(t * ATT, ATT)
                page = kv_d[bass.ds(h, 1)].rearrange("o c t -> (o c) t")
                sp.dma_start(kT[:], page[0:C, col]).then_inc(d_att, 16)
                sp.dma_start(vT[:], page[C:2 * C, col]).then_inc(d_att, 16)
                sp.dma_start(ya[:], yT_d[:, col]).then_inc(d_att, 16)
                sp.dma_start(wqh[:], wq[bass.ds(h, 1)].rearrange("o c k -> (o c) k")).then_inc(d_att, 16)

            def store_kv(n):
                m = n - 1 + NBLK
                h, blk = m // NBLK, m % NBLK
                sp.wait_ge(s["kv_sb"], n + 1)
                sp.dma_start(kv_d[bass.ds(h, 1)].rearrange("o c t -> (o c) t")[:, bass.ds(blk * BLK, BLK)],
                             kv_s[:]).then_inc(d_kv, 16)

            def store_o(n):
                m = n - LAG + NBLK
                h, t = m // NBLK, m % NBLK
                sp.wait_ge(s["o_sb"], n + 2)
                sp.dma_start(o_d[bass.ds(h, 1)].rearrange("o c t -> (o c) t")[:, bass.ds(t * ATT, ATT)],
                             oT[:]).then_inc(d_o, 16)

            for k in range(4):
                load_table(0, k)
            load_selection(0)
            sp.wait_ge(s["sims"], 1)
            load_selection(1)
            move_pairs(0, 0)
            load_attention(0)
            with sp.Fori(0, HEADS) as h:
                with sp.Fori(0, NBLK // 2) as i:
                    for p in range(2):
                        g = h * NBLK + i * 2 + p
                        store_kv(g)
                        sp.wait_ge(s["sims"], g + 2)
                        load_selection(g + 2)
                        move_pairs(g + 1, 1 - p)
                        sp.wait_ge(s["pv"], g + 1)
                        sp.wait_ge(d_kv, g * 16 + 32)
                        load_attention(g + 1)
                        store_o(g)
                for k in range(4):
                    sp.wait_ge(s["mixed"], h * (4 * NBLK) + (4 * NBLK - 2 + k))
                    load_table((h + 1) % HEADS, k)
            store_kv(STEPS)
            sp.wait_ge(d_kv, 16 * (STEPS + 2))
            for g in range(STEPS, STEPS + LAG):
                sp.wait_ge(s["pv"], g + 1)
                if g + 1 < STEPS + LAG:
                    load_attention(g + 1)
                store_o(g)
            for k in range(4):
                sp.wait_ge(d_tbl[k], 16 * (HEADS + 1))
            sp.wait_ge(d_sel, 32 * (STEPS + 2))
            sp.wait_ge(d_o, 16 * (STEPS + LAG + 1))

        @block.tensor
        def _(pe):
            def select(n, slot):
                if slot == 0:
                    pe.wait_ge(d_sel, n * 32 + 32)
                    if not first(n):
                        pe.wait_ge(s["split_sb"], n)
                    for t in range(TILES):
                        last = nc.tensor.matmul(A[:, t * 128:t * 128 + 128], yt[:, t * 128:t * 128 + 128], mh[:], start=True, stop=True)
                    last.then_inc(s["sims"], 1)
                if slot == 20:
                    pe.wait_ge(s["lo"], n + 1)
                    a16 = A[:].bitcast(f16)
                    for x, src in enumerate((sc_hi, sc_lo)):
                        for t in range(TILES):
                            last = nc.tensor.transpose(a16[:, x * BLK + t * 128:x * BLK + t * 128 + 128], src[:, t, :], ident16[:])
                    last.then_inc(s["turned"], 1)
                if slot in (23, 26, 28):
                    t = (23, 26, 28).index(slot)
                    pe.wait_ge(s_oh[t], n + 1)
                    for a in range(TOP):
                        last = nc.tensor.matmul(Bk[:, t * 128:t * 128 + 128], onehot[:, t, a, :], ident16[:],
                                                start=(a == 0), stop=(a == TOP - 1))
                    if t == TILES - 1:
                        last.then_inc(s["ranks_ps"], 1)

            def attend(n, slot):
                if slot == 2:
                    pe.wait_ge(d_att, n * 64 + 64)
                    hold(pe, s["o_sb"], n + 1, passed["pe"])
                    nc.tensor.matmul(Ck[0:C, 0:ATT], wqh[:], ya[:], start=True, stop=True).then_inc(s["q_ps"], 1)
                if slot == 3:
                    for k in range(2 * NB):
                        last = nc.tensor.transpose(Bk[0:HALF, k * C:(k + 1) * C], vT[:, k * HALF:(k + 1) * HALF], ident[0:C, 0:C])
                    last.then_inc(s["v_ps"], 1)
                if slot in (5, 6, 8):
                    b = (5, 6, 8).index(slot)
                    hold(pe, (s["q_sb"], s["v_sb"], s_msk[0])[b], n + 1, passed["pe"])
                    dst = (Ck, Bk, Ck)[b]
                    for a in range(2):
                        last = nc.tensor.matmul(dst[0:HALF, a * T:(a + 1) * T], qT[:, b * T + a * HALF:b * T + a * HALF + HALF],
                                                kT[:, b * T:(b + 1) * T], start=True, stop=True)
                    last.then_inc(s_sim[b], 1)
                if slot in (22, 24):
                    half = (22, 24).index(slot)
                    hold(pe, (s["att_p"], s["pt0_sb"])[half], n + 1, passed["pe"])
                    for b in ((0, 1), (2,))[half]:
                        col = (b % 2) * 198
                        for k, (a, j) in enumerate(((0, 0), (1, 0), (1, 1))):
                            last = nc.tensor.transpose(Ck[0:HALF, col + k * HALF:col + (k + 1) * HALF],
                                                       probn[:, 2 * b + a, j * HALF:(j + 1) * HALF], ident[0:HALF, 0:HALF])
                    last.then_inc(s[("pt0", "pt1")[half]], 1)
                if slot == 26:
                    hold(pe, s["pt1_sb"], n + 1, passed["pe"])
                    for b in range(NB):
                        nc.tensor.matmul(Ck[0:C, b * T:(b + 1) * T], v_s[:, 2 * b, :], pT[:, b * 198:b * 198 + T], start=True, stop=False)
                        last = nc.tensor.matmul(Ck[0:C, b * T + HALF:(b + 1) * T], v_s[:, 2 * b + 1, :],
                                                pT[:, b * 198 + T:b * 198 + 198], start=False, stop=True)
                    last.then_inc(s["pv"], 1)

            def mix(c):
                last = nc.tensor.matmul(kv_b[:, 0:BLK], tbl[:, c, :], wt[c % 4][:], start=(c == 0), stop=(c == CHUNKS - 1))
                if c % 8 == 7:
                    last.then_inc(s["mixed"], 1)

            for slot in range(32):
                select(0, slot)
            pe.wait_ge(d_tbl[3], 16)
            pe.wait_ge(s["weights"], 1)
            nc.tensor.matmul(kv_b[:, 0:BLK], tbl[:, 30, :], wt[2][:], start=True, stop=False)
            with pe.Fori(0, HEADS) as h:
                with pe.Fori(0, NBLK // 2) as i:
                    for p in range(2):
                        g = h * NBLK + i * 2 + p
                        for c in range(CHUNKS):
                            if c == 0:
                                pe.wait_ge(s["ranks_sb"], g + 1)
                                pe.wait_ge(d_pairs[p], (h * (NBLK // 2) + i) * 128 + 128)
                            pe.wait_ge(s["weights"], g * CHUNKS + (c + 1))
                            q = c // 8
                            nc.tensor.matmul(mask_b[c % 2][:, 0:BLK], sel_mask[:, c, :], ranks[p][:], start=True, stop=True)
                            nc.tensor.matmul(score_b[c % 2][:, 0:BLK], sel_score[:, c % 8, :], pairs[p][:, q // 2, q % 2, :],
                                             start=True, stop=True).then_inc(s["scores"], 1)
                            if c == 2:
                                pe.wait_ge(s["kv_sb"], g + 1)
                            if c % 8 == 2:
                                pe.wait_ge(d_tbl[c // 8], h * 16 + 16)
                            mix((c - 2) % CHUNKS)
                            select(g + 1, c)
                            attend(g, c)
            pe.wait_ge(s["weights"], STEPS * CHUNKS + 2)
            mix(30)
            mix(31)
            pe.wait_ge(s["ranks_sb"], STEPS + 1)
            for g in range(STEPS, STEPS + LAG):
                for slot in range(32):
                    attend(g, slot)

        @block.scalar
        def _(act):
            def select(n, slot):
                if slot == 1:
                    act.wait_ge(s["sims"], n + 1)
                    nc.scalar.activation(S[:].rearrange("p t a k -> p (t a k)"), A[:, 0:BLK], ACT.Copy).then_inc(s["sims_sb"], 1)
                if slot == 11:
                    act.wait_ge(s["idxs"], n + 1)
                    nc.scalar.activation(idxf[:], idx[:], ACT.Copy).then_inc(s["idxf_sb"], 1)
                if slot == 14:
                    act.wait_ge(s["best_v"], n + 1)
                    nc.scalar.activation(norm[:, 0, :], best[:, :, 0], ACT.Copy, scale=-1.0)
                    act.drain()
                    for t in range(TILES):
                        nc.scalar.activation(junk[:, t, :], best[:, t, :], ACT.Exp, bias=norm[:, 0, t:t + 1], accum_out=norm[:, 1, t:t + 1])
                    act.drain()
                    nc.scalar.activation(norm[:, 2, :], norm[:, 1, :], ACT.Ln).then_inc(s["lnz"], 1)
                if slot == 17:
                    act.wait_ge(s["shifted"], n + 1)
                    nc.scalar.activation(sc_hi[:], sc[:].rearrange("p t a k -> p t (a k)"), ACT.Copy).then_inc(s["hi"], 1)
                if slot == 21:
                    act.wait_ge(s["turned"], n + 1)
                    if not first(n):
                        act.wait_ge(d_pairs[n_parity[0]], moved[0])
                    nc.scalar.activation(split[:].rearrange("p x t -> p (x t)"), A[:].bitcast(f16)[:, 0:2 * BLK], ACT.Copy).then_inc(s["split_sb"], 1)
                if slot == 29:
                    act.wait_ge(s["ranks_ps"], n + 1)
                    nc.scalar.activation(ranks[n_parity[1]][:], Bk[:, 0:BLK], ACT.Copy).then_inc(s["ranks_sb"], 1)

            n_parity, moved = [1, 0], [None]

            def attend(n, slot):
                if slot == 3:
                    act.wait_ge(s["q_ps"], n + 1)
                    nc.scalar.activation(qT[:], Ck[0:C, 0:ATT], ACT.Copy, scale=C ** -0.5).then_inc(s["q_sb"], 1)
                if slot == 4:
                    act.wait_ge(s["v_ps"], n + 1)
                    nc.scalar.activation(v_s[:].rearrange("p k c -> p (k c)"), Bk[0:HALF, 0:2 * NB * C], ACT.Copy).then_inc(s["v_sb"], 1)
                if 12 <= slot < 18:
                    k = slot - 12
                    if k == 0:
                        act.wait_ge(s["negmax"], n + 1)
                    last = nc.scalar.activation(prob[:, k, :], sim[:, k, :], ACT.Exp, bias=negmax[:, k:k + 1], accum_out=psum_[:, k:k + 1])
                    if k == 5:
                        last.then_inc(s["att_exp"], 1)
                if slot == 23:
                    act.wait_ge(s["pt0"], n + 1)
                    nc.scalar.activation(pT[:, 0:396], Ck[0:HALF, 0:396], ACT.Copy).then_inc(s["pt0_sb"], 1)
                if slot == 25:
                    act.wait_ge(s["pt1"], n + 1)
                    nc.scalar.activation(pT[:, 396:594], Ck[0:HALF, 0:198], ACT.Copy).then_inc(s["pt1_sb"], 1)
                if slot == 27:
                    act.wait_ge(s["pv"], n + 1)
                    act.wait_ge(d_o, n * 16 + 16)
                    nc.scalar.activation(oT[:], Ck[0:C, 0:ATT], ACT.Copy).then_inc(s["o_sb"], 1)

            def evacuate_kv(n):
                act.wait_ge(s["mixed"], n * 4 + 1)
                act.wait_ge(d_kv, n * 16 + 16)
                nc.scalar.activation(kv_s[:], kv_b[:, 0:BLK], ACT.Copy).then_inc(s["kv_sb"], 1)

            act.sem_inc(s["o_sb"], 1)
            act.dma_start(oT[:], yT_d[:, 0:ATT]).then_inc(d_o, 16)
            act.dma_start(kv_s[:], kv_d[0][:, 0:BLK]).then_inc(d_kv, 16)
            for slot in range(32):
                select(0, slot)
            with act.Fori(0, HEADS) as h:
                with act.Fori(0, NBLK // 2) as i:
                    for p in range(2):
                        g = h * NBLK + i * 2 + p
                        n_parity[:] = [p, 1 - p]
                        moved[0] = (h * (NBLK // 2) + i) * 128 + 128
                        for c in range(CHUNKS):
                            act.wait_ge(s["scores"], g * CHUNKS + (c + 1))
                            nc.scalar.activation(ex[c % 2][:], score_b[c % 2][:, 0:BLK], ACT.Exp).then_inc(s["probs"], 1)
                            if c == 1:
                                evacuate_kv(g)
                            select(g + 1, c)
                            attend(g, c)
            evacuate_kv(STEPS)
            for g in range(STEPS, STEPS + LAG):
                for slot in range(32):
                    attend(g, slot)

        @block.vector
        def _(dve):
            def select(n, slot):
                if slot in (2, 3):
                    if slot == 2:
                        hold(dve, s["sims_sb"], n + 1, passed["dve"])
                    for t, a in GROUPS[slot - 2]:
                        nc.vector.max(val[:, t, a, 0:8], S[:, t, a, :])
                if slot in (4, 5, 6):
                    if slot == 4:
                        dve.drain()
                    for t, a in PARTS[slot - 4]:
                        nc.vector.max_index(idx[:, t, a, 0:8], val[:, t, a, 0:8], S[:, t, a, :])
                        nc.vector.match_replace(S2[:, t, a, :], val[:, t, a, 0:8], S[:, t, a, :], LOWEST)
                if slot in (7, 8):
                    if slot == 7:
                        dve.drain()
                    for t, a in GROUPS[slot - 7]:
                        last = nc.vector.max(val[:, t, a, 8:16], S2[:, t, a, :])
                    if slot == 8:
                        last.then_inc(s["vals"], 1)
                if slot in (9, 10):
                    if slot == 9:
                        dve.drain()
                    for t, a in GROUPS[slot - 9]:
                        last = nc.vector.max_index(idx[:, t, a, 8:16], val[:, t, a, 8:16], S2[:, t, a, :])
                    if slot == 10:
                        last.then_inc(s["idxs"], 1)
                if slot in (11, 13):
                    if slot == 11:
                        hold(dve, s["cands"], n + 1, passed["dve"])
                    else:
                        dve.drain()
                    k = (slot - 11) // 2
                    for t in range(TILES):
                        last = nc.vector.max(best[:, t, 8 * k:8 * k + 8], (cand, cand1)[k][:, t, :])
                    if k == 1:
                        last.then_inc(s["best_v"], 1)
                if slot in (12, 14):
                    dve.drain()
                    k = (slot - 12) // 2
                    for t in range(TILES):
                        nc.vector.match_replace((cand1, cand2)[k][:, t, :], best[:, t, 8 * k:8 * k + 8], (cand, cand1)[k][:, t, :], LOWEST)
                if slot == 15:
                    dve.drain()
                    nc.vector.tensor_tensor(picked[:], cand2[:], cand[:], ALU.not_equal)
                if slot == 16:
                    dve.drain()
                    for a, rows, cols, at in CAND:
                        src = picked[:, :, at:at + rows * cols].rearrange("p t (a b) -> p t a b", a=rows)
                        if cols > 1:
                            nc.vector.tensor_reduce(kept[:, :, a:a + rows], src, AX.X, ALU.add)
                        else:
                            nc.vector.tensor_copy(kept[:, :, a:a + rows], picked[:, :, at:at + rows])
                if 12 <= slot < 28:
                    if slot == 12:
                        dve.wait_ge(s["idxf_sb"], n + 1)
                        if not first(n):
                            dve.wait_ge(s["ranks_ps"], n)
                    if slot == 20:
                        dve.drain()
                    for k in range(6 * (slot - 12), 6 * (slot - 12) + 6):
                        if k < 48:
                            t, a = k // 16, k % 16
                            nc.vector.tensor_scalar(onehot[:, t, a, NK:], iota16[:], idxf[:, t, 1, a:a + 1], float(TOP - a), ALU.is_equal, ALU.mult)
                        else:
                            t, a = (k - 48) // 16, k % 16
                            last = nc.vector.tensor_scalar(onehot[:, t, a, 0:NK], iota16[:], idxf[:, t, 0, a:a + 1], kept[:, t, a:a + 1], ALU.is_equal, ALU.mult)
                            if a == 15:
                                last.then_inc(s_oh[t], 1)

            GROUPS = [[(0, 0), (0, 1), (1, 0)], [(1, 1), (2, 0), (2, 1)]]
            PARTS = [[(0, 0), (0, 1)], [(1, 0), (1, 1)], [(2, 0), (2, 1)]]

            def attend(n, slot):
                if slot in (6, 7, 9):
                    b = (6, 7, 9).index(slot)
                    dve.wait_ge(s_sim[b], n + 1)
                    src = (Ck, Bk, Ck)[b]
                    nc.vector.tensor_tensor(sim[:, 2 * b:2 * b + 2, :].rearrange("p a t -> p (a t)"), src[0:HALF, 0:2 * T],
                                            causal[:].rearrange("p a t -> p (a t)"), ALU.add).then_inc(s_msk[b], 1)
                if slot == 10:
                    dve.wait_ge(s_msk[2], n + 1)
                    nc.vector.tensor_reduce(negmax[:], sim[:], AX.X, ALU.max, negate=True).then_inc(s["negmax"], 1)
                if slot == 18:
                    dve.wait_ge(s["att_exp"], n + 1)
                    nc.vector.reciprocal(prec[:], psum_[:]).then_inc(s["att_rec"], 1)

            for k in (2, 3):
                nc.vector.memset(wt[k][:], 0.0).then_inc(s["weights"], 1)
            for slot in range(32):
                select(0, slot)
            with dve.Fori(0, HEADS) as h:
                with dve.Fori(0, NBLK // 2) as i:
                    for p in range(2):
                        g = h * NBLK + i * 2 + p
                        for c in range(CHUNKS):
                            dve.wait_ge(s["probs"], g * CHUNKS + (c + 1))
                            nc.vector.scalar_tensor_tensor(out=wt[c % 4][:], in0=mask_b[c % 2][:, 0:BLK], scalar=float(TOP), in1=ex[c % 2][:],
                                                           op0=ALU.is_gt, op1=ALU.mult).then_inc(s["weights"], 1)
                            select(g + 1, c)
                            attend(g, c)
            for g in range(STEPS, STEPS + LAG):
                for slot in range(32):
                    attend(g, slot)

        @block.gpsimd
        def _(pool):
            def select(n, slot):
                if slot == 9:
                    pool.wait_ge(s["vals"], n + 1)
                    for a, rows, cols, at in CAND:
                        out = cand[:, :, at:at + rows * cols].rearrange("p t (a b) -> p t a b", a=rows)
                        one = val[:, :, 0, a:a + rows].unsqueeze(3).broadcast_to([128, TILES, rows, cols])
                        two = val[:, :, 1, 0:cols].unsqueeze(2).broadcast_to([128, TILES, rows, cols])
                        last = pool.tensor_tensor(out, one, two, ALU.add)
                    last.then_inc(s["cands"], 1)
                if slot == 15:
                    pool.wait_ge(s["lnz"], n + 1)
                    pool.tensor_tensor(norm[:, 3, :], val[:, :, 0, 0], norm[:, 2, :], ALU.add)
                    pool.drain()
                    for t in range(TILES):
                        pool.tensor_scalar(sc[:, t, 0, :], S[:, t, 0, :], norm[:, 3, t:t + 1], FLOOR, ALU.subtract, ALU.max)
                        last = pool.tensor_scalar(sc[:, t, 1, :], S[:, t, 1, :], val[:, t, 1, 0:1], FLOOR, ALU.subtract, ALU.max)
                    last.then_inc(s["shifted"], 1)
                if slot == 18:
                    pool.wait_ge(s["hi"], n + 1)
                    pool.tensor_tensor(sc_lo[:], sc[:].rearrange("p t a k -> p t (a k)"), sc_hi[:], ALU.subtract).then_inc(s["lo"], 1)

            def attend(n, slot):
                if slot == 19:
                    pool.wait_ge(s["att_rec"], n + 1)
                    pool.tensor_tensor(probn[:], prob[:], prec[:].unsqueeze(2).broadcast_to([HALF, 2 * NB, T]), ALU.mult).then_inc(s["att_p"], 1)

            for slot in range(32):
                select(0, slot)
            with pool.Fori(0, STEPS) as g:
                for slot in range(32):
                    select(g + 1, slot)
                    attend(g, slot)
            for g in range(STEPS, STEPS + LAG):
                for slot in range(32):
                    attend(g, slot)


def final(nc, ctx, sb, sem, bank, env):
    f32 = env["f32"]
    ALU = env["ALU"]
    h1_d, o_d, wo, out = env["h1_d"], env["o_d"], env["wo"], env["out"]
    passed = env["passed"]
    with ExitStack() as local:
        def sb(name, shape, dt=f32):
            return local.enter_context(nc.sbuf_tensor(name, shape, dt))

        wo_s = sb("wo_s", [128, 4, C])
        ob = [sb(f"ob{p}", [128, 4, BLK]) for p in range(2)]
        hb = [sb(f"hb{p}", [128, TILES, C]) for p in range(2)]
        res = [sb(f"res{p}", [128, TILES, C]) for p in range(2)]
        f_wo, f_mm, f_res = sem("f_wo"), sem("f_mm"), sem("f_res")
        f_in = [sem(f"f_in{p}") for p in range(2)]
        f_out = [sem(f"f_out{p}") for p in range(2)]
        o_v = o_d[1:HEADS + 1].rearrange("(k e) c t -> (e c) k t", e=2)
        h_v = h1_d.rearrange("(n k p) c -> p n k c", k=TILES, p=128)
        out_v = out.rearrange("b t c -> (b t) c").rearrange("(n k p) c -> p n k c", k=TILES, p=128)
        block = local.enter_context(nc.Block())

        @block.sync
        def _(sp):
            def load(n, p):
                sp.dma_start(ob[p][:], o_v[:, :, bass.ds(n * BLK, BLK)]).then_inc(f_in[p], 16)
                sp.dma_start(hb[p][:], h_v[:, bass.ds(n, 1)].rearrange("p o k c -> p (o k) c")).then_inc(f_in[p], 16)

            def store(n, p):
                sp.dma_start(out_v[:, bass.ds(n, 1)].rearrange("p o k c -> p (o k) c"), res[p][:]).then_inc(f_out[p], 16)

            sp.dma_start(wo_s[:], wo.rearrange("(k p) c -> p k c", p=128)).then_inc(f_wo, 16)
            load(0, 0)
            load(1, 1)
            with sp.Fori(0, NBLK // 2 - 1) as i:
                for p in range(2):
                    sp.wait_ge(f_res, i * 2 + (p + 1))
                    store(i * 2 + p, p)
                    load(i * 2 + (p + 2), p)
            for p in range(2):
                sp.wait_ge(f_res, NBLK - 1 + p)
                store(NBLK - 2 + p, p)
            for p in range(2):
                sp.wait_ge(f_out[p], 16 * (NBLK // 2))

        @block.tensor
        def _(pe):
            pe.wait_ge(f_wo, 16)

            def block_of(n, i, p):
                pe.wait_ge(f_in[p], i * 32 + 32)
                if n is not None:
                    pe.wait_ge(f_res, n)
                for t in range(TILES):
                    for k in range(4):
                        last = nc.tensor.matmul(bank[p][:, t * C:(t + 1) * C], ob[p][:, k, t * 128:(t + 1) * 128],
                                                wo_s[:, k, :], start=(k == 0), stop=(k == 3))
                last.then_inc(f_mm, 1)

            for p in range(2):
                block_of(None, 0, p)
            with pe.Fori(1, NBLK // 2) as i:
                for p in range(2):
                    block_of(i * 2 + (p - 1), i, p)

        @block.vector
        def _(dve):
            def block_of(i, p, again):
                dve.wait_ge(f_mm, i * 2 + (p + 1))
                if again:
                    dve.wait_ge(f_out[p], i * 16)
                nc.vector.tensor_tensor(res[p][:].rearrange("p k c -> p (k c)"), bank[p][:, 0:TILES * C],
                                        hb[p][:].rearrange("p k c -> p (k c)"), ALU.add).then_inc(f_res, 1)

            for p in range(2):
                block_of(0, p, False)
            with dve.Fori(1, NBLK // 2) as i:
                for p in range(2):
                    block_of(i, p, True)


_OUTS = [((B, T, C), "float32")]


def kernel(x, txt, L0_tok_weight, L0_tok_bias, L0_attn_time_w, L0_attn_time_mix_k, L0_attn_time_mix_v,
           L0_attn_time_mix_r, L0_attn_Wk, L0_attn_Wv, L0_attn_Wr, L0_attn_Wo, L0_ffn_Wq_pk, L0_ffn_pk_keys,
           L0_ffn_Wq, L0_ffn_keys_table, L0_ffn_values_table, L0_ffn_Wo):
    import numpy as _np
    import concourse.bacc as _bacc
    from concourse import mybir as _mybir
    from concourse.bass_utils import run_bass_kernel_spmd as _run

    a = _np.asarray
    late = a(L0_attn_time_w)[::-1]
    distance = _np.abs(_np.arange(T)[None, :] - _np.arange(T)[:, None])
    mix = _np.stack([a(m).reshape(C) for m in (L0_attn_time_mix_k, L0_attn_time_mix_v, L0_attn_time_mix_r)], axis=1)
    wkvr = _np.concatenate([a(L0_attn_Wk), a(L0_attn_Wv), a(L0_attn_Wr)], axis=1)

    def rows(tab):
        return a(tab).reshape(HEADS, 2, 32, 2, 8, 4, C).transpose(0, 5, 2, 3, 1, 4, 6).reshape(HEADS, 128, CHUNKS, C)

    wq = a(L0_ffn_Wq).reshape(C, HEADS, C).transpose(1, 0, 2)
    ins = {
        "x": a(x), "txt": a(txt), "tok_w": a(L0_tok_weight), "tok_b": a(L0_tok_bias),
        "toeplitz": late[distance],
        "mix": _np.concatenate([mix, mix], axis=0), "wkvr": _np.concatenate([wkvr, wkvr], axis=0),
        "attn_wo": a(L0_attn_Wo),
        "wqT": a(L0_ffn_Wq_pk).reshape(C, 2, HEADS, DK).transpose(3, 2, 1, 0).reshape(DK, 2 * HEADS, C),
        "keysT": a(L0_ffn_pk_keys).transpose(3, 2, 0, 1).reshape(DK, 2 * HEADS, NK),
        "wq": _np.concatenate([wq[:1], wq], axis=0),
        "table": _np.concatenate([rows(L0_ffn_keys_table), rows(L0_ffn_values_table)], axis=3),
        "wo": a(L0_ffn_Wo),
    }
    nc = _bacc.Bacc("TRN2", target_bir_lowering=False, num_devices=1)
    arrays, args = {}, []
    for name, v in ins.items():
        v = _np.ascontiguousarray(v)
        arrays[f"in_{name}"] = v
        args.append(nc.dram_tensor(f"in_{name}", v.shape, _mybir.dt.from_np(v.dtype), kind="ExternalInput").ap())
    shape, dtype = _OUTS[0]
    args.append(nc.dram_tensor("out_0", shape, _mybir.dt.from_np(_np.dtype(dtype)), kind="ExternalOutput").ap())
    build(nc, *args)
    r = _run(nc, [arrays], core_ids=[0])
    return r.results[0]["out_0"]
```

```python
import numpy as np
import concourse.bass as bass
from concourse import mybir
from contextlib import ExitStack

B, T, C = 64, 132, 64
NIMG, TXT = 4, 128
PH, PW, SW = 64, 25, 12
HALF = T // 2
N = B * T
HEADS, NK, TOP = 8, 64, 16
DK = 32
BLK, TILES = 384, 3
NBLK = N // BLK
NB = 3
ATT = NB * T
NPAD = NBLK * ATT
CHUNKS = NK * NK // 128
GRP = 4
STEPS = HEADS * NBLK
LAG = 3
AHEAD = 3
EPS = 1e-5
LOWEST = -3.4028234663852886e38
FLOOR = -60000.0
CAND = [(0, 1, 16, 0), (1, 3, 8, 16), (4, 4, 4, 40), (8, 8, 1, 56)]
NCAND = 64


def hold(eng, semaphore, value, passed):
    eng.wait_ge(semaphore, value)
    eng.sem_inc(passed, 1)


def build(nc, x, txt, tok_w, tok_b, toeplitz, mix, wkvr, attn_wo, wqT, keysT, wq, table, wo, out):
    f32, f16, u32 = mybir.dt.float32, mybir.dt.float16, mybir.dt.uint32
    ALU, ACT, AX = mybir.AluOpType, mybir.ActivationFunctionType, mybir.AxisListType
    ctx = ExitStack()
    with ctx:
        def sb(name, shape, dt=f32):
            return ctx.enter_context(nc.sbuf_tensor(name, shape, dt))

        def sem(name):
            return ctx.enter_context(nc.semaphore(name))

        bank = [ctx.enter_context(nc.psum_tensor(f"bank{i}", [128, 512], f32)) for i in range(8)]

        h0_d = nc.dram_tensor("h0_d", (B * NIMG, C), f32, kind="Internal").ap()
        h1_d = nc.dram_tensor("h1_d", (N, C), f32, kind="Internal").ap()
        yT_d = nc.dram_tensor("yT_d", (C, NPAD), f32, kind="Internal").ap()
        m_d = nc.dram_tensor("m_d", (HEADS + 1, C, 2 * NK), f32, kind="Internal").ap()
        kv_d = nc.dram_tensor("kv_d", (HEADS + 1, 2 * C, NPAD), f32, kind="Internal").ap()
        o_d = nc.dram_tensor("o_d", (HEADS + 1, C, NPAD), f32, kind="Internal").ap()

        ident = sb("ident", [128, 128])
        ident16 = sb("ident16", [128, 128], f16)
        sel_mask = sb("sel_mask", [128, CHUNKS, 128], f16)
        sel_score = sb("sel_score", [128, 8, 128], f16)
        key_of = sb("key_of", [128, NK, TOP], f16)
        from_top = sb("from_top", [128, TOP], f16)
        causal = sb("causal", [HALF, 2, T])
        s_const = sem("s_const")
        passed = {e: sem("passed_" + e) for e in ("pe", "dve", "sp")}

        front(nc, ctx, sb, sem, bank, locals())
        main(nc, ctx, sb, sem, bank, locals())
        final(nc, ctx, sb, sem, bank, locals())


def front(nc, ctx, sb, sem, bank, env):
    f32, f16 = env["f32"], env["f16"]
    ALU, ACT, AX = env["ALU"], env["ACT"], env["AX"]
    x, txt, out = env["x"], env["txt"], env["out"]
    h0_d, h1_d, yT_d, m_d, kv_d = (env[k] for k in ("h0_d", "h1_d", "yT_d", "m_d", "kv_d"))
    ident, ident16, sel_mask, sel_score = (env[k] for k in ("ident", "ident16", "sel_mask", "sel_score"))
    key_of, from_top, causal, s_const = env["key_of"], env["from_top"], env["causal"], env["s_const"]
    passed = env["passed"]
    with ExitStack() as local:
        def sb(name, shape, dt=f32):
            return local.enter_context(nc.sbuf_tensor(name, shape, dt))

        img = sb("img", [PH, B, C])
        patch_w = sb("patch_w", [PH, PW, C])
        patch_b = sb("patch_b", [C, 1])
        h0T = sb("h0T", [C, B * NIMG])
        h0 = sb("h0", [128, 2, C])
        wmix = sb("wmix", [128, 3, C])
        mixc = sb("mixc", [128, 3])
        wo1 = sb("wo1", [C, C])
        wT = sb("wT", [HALF, 2, T])
        tri = sb("tri", [HALF, 2, T])
        wqT_s = sb("wqT_s", [DK, 2 * HEADS, C])
        keysT_s = sb("keysT_s", [DK, 2 * HEADS, NK])
        m_s = sb("m_s", [C, 2 * HEADS * NK])
        zeros = sb("zeros", [128, NPAD])
        X = sb("X", [HALF, 2, GRP, C])
        XC = sb("XC", [HALF, 2 * GRP, C])
        SQ = sb("SQ", [HALF, 2 * GRP, C])
        Y = sb("Y", [HALF, 2, GRP, 2, C])
        stat = sb("stat", [HALF, 4, 2 * GRP])
        XT = sb("XT", [128, GRP, T + 1])
        KC = sb("KC", [HALF, 2, GRP, C])
        K = sb("K", [HALF, 2, GRP, C])
        KV = sb("KV", [HALF, 2, GRP, C])
        ER = sb("ER", [HALF, 2, GRP, C])
        DEN = sb("DEN", [HALF, 2 * GRP, C])
        RW = sb("RW", [HALF, 2, GRP, C])
        RWT = sb("RWT", [C, GRP, T])
        H1 = sb("H1", [HALF, 2, GRP, C])
        YT = sb("YT", [C, GRP, T])

        s_img = sem("s_img")
        s_wload = sem("s_wload")
        s_mload = sem("s_mload")
        s_patch, s_gelu, s_h0T, s_h0, s_h0_st = (sem(n) for n in ("s_patch", "s_gelu", "s_h0T", "s_h0", "s_h0_st"))
        s_wready, s_m, s_m_sb, s_m_st, s_zero, s_zero_st = (sem(n) for n in ("s_wready", "s_m", "s_m_sb", "s_m_st", "s_zero", "s_zero_st"))
        s_xin = sem("s_xin")
        s_cen = [sem(f"s_cen{i}") for i in range(2)]
        s_sq = [sem(f"s_sq{i}") for i in range(2)]
        s_var = [sem(f"s_var{i}") for i in range(2)]
        s_std = [sem(f"s_std{i}") for i in range(2)]
        s_norm = [sem(f"s_norm{i}") for i in range(2)]
        s_turn = [sem(f"s_turn{i}") for i in range(2)]
        s_xt, s_proj, s_clip, s_exp, s_kv, s_mix, s_rw, s_rwt, s_rwt_sb, s_ao, s_h1, s_h1_st, s_yt, s_yt_st = (
            sem(n) for n in ("s_xt", "s_proj", "s_clip", "s_exp", "s_kv", "s_mix", "s_rw", "s_rwt",
                             "s_rwt_sb", "s_ao", "s_h1", "s_h1_st", "s_yt", "s_yt_st"))

        groups = B // GRP
        def turned(rows, k):
            return bank[k][rows, 0:2 * T].rearrange("p (b t) -> p b t", b=2)

        block = local.enter_context(nc.Block())

        @block.sync
        def _(sp):
            with nc.allow_non_contiguous_dma(reason="rows of 256 bytes"):
                sp.dma_start(img[:], x.rearrange("b c h w -> h (b c) w")).then_inc(s_img, 16)
                sp.dma_start(patch_w[:], env["tok_w"].rearrange("(h w) d -> h w d", h=PH)).then_inc(s_img, 16)
                sp.dma_start(patch_b[:], env["tok_b"].rearrange("(d o) -> d o", o=1)).then_inc(s_img, 16)
                sp.dma_start(wmix[:].rearrange("p a b -> p (a b)"), env["wkvr"]).then_inc(s_wload, 16)
                sp.dma_start(mixc[:], env["mix"]).then_inc(s_wload, 16)
                sp.dma_start(wo1[:], env["attn_wo"]).then_inc(s_wload, 16)
                sp.dma_start(wT[:], env["toeplitz"].rearrange("(a u) t -> u a t", a=2)).then_inc(s_wload, 16)
                sp.dma_start(wqT_s[:], env["wqT"]).then_inc(s_mload, 16)
                sp.dma_start(keysT_s[:], env["keysT"]).then_inc(s_mload, 16)
                sp.wait_ge(s_zero, 1)
                sp.dma_start(kv_d[0], zeros[:]).then_inc(s_zero_st, 16)
                for h in range(1, HEADS + 1):
                    sp.dma_start(kv_d[h][:, N:NPAD], zeros[:, 0:NPAD - N]).then_inc(s_zero_st, 16)
                sp.dma_start(yT_d[:, N:NPAD], zeros[0:C, 0:NPAD - N]).then_inc(s_zero_st, 16)
                sp.wait_ge(s_m_sb, 1)
                for h in range(HEADS + 1):
                    sp.dma_start(m_d[h], m_s[:, 128 * (h % HEADS):128 * (h % HEADS) + 128]).then_inc(s_m_st, 16)
                sp.wait_ge(s_h0, 1)
                sp.dma_start(h0_d.rearrange("(k p) d -> p k d", k=2), h0[:]).then_inc(s_h0_st, 16)
                sp.wait_ge(s_h0_st, 16)
                h0_v = h0_d.rearrange("(b n) d -> n b d", n=NIMG)
                txt_v = txt.rearrange("b t d -> t b d")
                h1_v = h1_d.rearrange("(b a t) d -> t a b d", a=2, t=HALF)
                yT_v = yT_d[:, 0:N].rearrange("c (b t) -> c b t", t=T)
                with sp.Fori(0, groups) as g:
                    b = bass.ds(g * GRP, GRP)
                    sp.dma_start(X[0:NIMG, 0], h0_v[:, b, :]).then_inc(s_xin, 16)
                    sp.dma_start(X[NIMG:HALF, 0], txt_v[0:HALF - NIMG, b, :]).then_inc(s_xin, 16)
                    sp.dma_start(X[:, 1], txt_v[HALF - NIMG:TXT, b, :]).then_inc(s_xin, 16)
                    sp.wait_ge(s_h1, g + 1)
                    for a in range(2):
                        sp.dma_start(h1_v[:, a, b, :], H1[:, a]).then_inc(s_h1_st, 16)
                    sp.wait_ge(s_yt, g + 1)
                    sp.dma_start(yT_v[:, b, :], YT[:]).then_inc(s_yt_st, 16)
                    sp.wait_ge(s_h1_st, g * 32 + 32)
                    hold(sp, s_yt_st, g * 16 + 16, passed["sp"])
                sp.wait_ge(s_zero_st, 16 * (HEADS + 2))
                sp.wait_ge(s_m_st, 16 * (HEADS + 1))

        @block.gpsimd
        def _(pool):
            pool.memset(zeros[:], 0.0).then_inc(s_zero, 1)
            pool.memset(ident[:], 0.0)
            pool.memset(ident16[:], 0.0)
            pool.memset(tri[:], 1.0)
            pool.memset(sel_mask[:], 0.0)
            pool.memset(sel_score[:], 0.0)
            pool.memset(causal[:], 0.0)
            pool.iota(key_of[:], [[1, NK], [0, TOP]], base=0, channel_multiplier=0, allow_small_or_imprecise_dtypes=True)
            pool.iota(from_top[:], [[-1, TOP]], base=TOP, channel_multiplier=0, allow_small_or_imprecise_dtypes=True)
            pool.drain()

            def one_where_zero(tile, pattern, base):
                pool.affine_select(out=tile, in_=tile, compare_op=ALU.not_equal, fill=1.0, base=base,
                                   pattern=pattern, channel_multiplier=1)

            one_where_zero(ident[:], [[-1, 128]], 0)
            one_where_zero(ident16[:], [[-1, 128]], 0)
            pool.wait_ge(s_wload, 64)
            for a in range(2):
                for w in (tri, wT):
                    pool.affine_select(out=w[:, a, :], in_=w[:, a, :], compare_op=ALU.is_ge, fill=0.0,
                                       base=-HALF * a, pattern=[[1, T]], channel_multiplier=-1)
                pool.affine_select(out=causal[:, a, :], in_=causal[:, a, :], compare_op=ALU.is_ge, fill=LOWEST,
                                   base=HALF * a, pattern=[[-1, T]], channel_multiplier=1)
            sm = sel_mask[:].rearrange("r (q c) (a b) -> r q c a b", q=4, a=4)
            for q in range(4):
                one_where_zero(sm[:, q], [[-4, 8], [-1, 4], [0, 32]], -32 * (q // 2))
            ss = sel_score[:].rearrange("r c (a b) -> r c a b", a=4)
            pool.drain()
            for q in range(4):
                one_where_zero(sm[:, q], [[0, 8], [0, 4], [-1, 32]], -64 - 32 * (q % 2))
            for k in range(2):
                one_where_zero(ss, [[0, 8], [0, 4], [-1, 32]], -32 * k)
                pool.drain()
                one_where_zero(ss, [[-4, 8], [-1, 4], [0, 32]], -64 - 32 * k)
                pool.drain()
            pool.drain().then_inc(s_const, 1)

        @block.tensor
        def _(pe):
            pe.wait_ge(s_img, 48)
            for w in range(PW):
                last = nc.tensor.matmul(bank[0][0:C, 0:B * NIMG].rearrange("d (b n) -> d b n", n=NIMG),
                                        patch_w[:, w, :], img[:, :, w:w + SW * (NIMG - 1) + 1:SW],
                                        start=(w == 0), stop=(w == PW - 1))
            last.then_inc(s_patch, 1)
            pe.wait_ge(s_mload, 32)
            for k in range(2 * HEADS):
                last = nc.tensor.matmul(bank[2 + k // 8][0:C, (k % 8) * NK:(k % 8) * NK + NK],
                                        wqT_s[:, k, :], keysT_s[:, k, :], start=True, stop=True)
            last.then_inc(s_m, 1)
            pe.wait_ge(s_const, 1)
            pe.wait_ge(s_gelu, 1)
            for k in range(2):
                last = nc.tensor.transpose(bank[1][:, k * C:(k + 1) * C], h0T[:, k * 128:(k + 1) * 128], ident[0:C, 0:C])
            last.then_inc(s_h0T, 1)
            pe.wait_ge(s_wready, 1)
            pe.wait_ge(s_m_sb, 1)
            pe.wait_ge(s_h0, 1)
            with pe.Fori(0, groups) as g:
                v = g + 1
                hold(pe, s_norm[0], v, passed["pe"])
                for b in range(GRP):
                    for a in range(2):
                        last = nc.tensor.transpose(turned(slice(0, 128), b // 2)[:, b % 2, a * HALF:(a + 1) * HALF],
                                                   Y[:, a, b].rearrange("p d c -> p (d c)"), ident[0:HALF, 0:HALF])
                last.then_inc(s_turn[0], 1)
                pe.wait_ge(s_xt, v)
                for b in range(GRP):
                    for a in range(2):
                        last = nc.tensor.matmul(bank[2 + b][0:HALF, a * 192:a * 192 + 192],
                                                XT[:, b, a * HALF:(a + 1) * HALF], wmix[:].rearrange("p a b -> p (a b)"),
                                                start=True, stop=True)
                last.then_inc(s_proj, 1)
                pe.wait_ge(s_kv, v)
                for w, src, bk in ((wT, KV, 6), (tri, K, 7)):
                    dst = bank[bk][0:HALF, :]
                    rows = [src[:, u].rearrange("p b c -> p (b c)") for u in range(2)]
                    nc.tensor.matmul(dst[:, 0:256], w[:, 0, 0:HALF], rows[0], start=True, stop=True)
                    nc.tensor.matmul(dst[:, 256:512], w[:, 0, HALF:T], rows[0], start=True, stop=False)
                    last = nc.tensor.matmul(dst[:, 256:512], w[:, 1, HALF:T], rows[1], start=False, stop=True)
                last.then_inc(s_mix, 1)
                hold(pe, s_rw, v, passed["pe"])
                for b in range(GRP):
                    for a in range(2):
                        last = nc.tensor.transpose(turned(slice(0, C), b // 2)[:, b % 2, a * HALF:(a + 1) * HALF],
                                                   RW[:, a, b], ident[0:HALF, 0:HALF])
                last.then_inc(s_rwt, 1)
                hold(pe, s_rwt_sb, v, passed["pe"])
                for b in range(GRP):
                    for a in range(2):
                        k = a * GRP + b
                        last = nc.tensor.matmul(bank[2][0:HALF, k * C:(k + 1) * C], RWT[:, b, a * HALF:(a + 1) * HALF],
                                                wo1[:], start=True, stop=True)
                last.then_inc(s_ao, 1)
                hold(pe, s_norm[1], v, passed["pe"])
                for b in range(GRP):
                    for a in range(2):
                        last = nc.tensor.transpose(turned(slice(0, C), b // 2)[:, b % 2, a * HALF:(a + 1) * HALF],
                                                   Y[:, a, b, 0], ident[0:HALF, 0:HALF])
                last.then_inc(s_turn[1], 1)

        @block.scalar
        def _(act):
            act.wait_ge(s_patch, 1)
            nc.scalar.activation(h0T[:], bank[0][0:C, 0:B * NIMG], ACT.Gelu, bias=patch_b[:, 0:1]).then_inc(s_gelu, 1)
            act.wait_ge(s_m, 1)
            nc.scalar.activation(m_s[:, 0:512], bank[2][0:C, :], ACT.Copy)
            nc.scalar.activation(m_s[:, 512:1024], bank[3][0:C, :], ACT.Copy).then_inc(s_m_sb, 1)
            act.wait_ge(s_h0T, 1)
            nc.scalar.activation(h0[:].rearrange("p k c -> p (k c)"), bank[1][:, 0:128], ACT.Copy).then_inc(s_h0, 1)
            act.wait_ge(s_wready, 1)
            with act.Fori(0, groups) as g:
                v = g + 1
                for n in range(2):
                    act.wait_ge(s_cen[n], v)
                    nc.scalar.activation(SQ[:], XC[:], ACT.Square).then_inc(s_sq[n], 1)
                    act.wait_ge(s_var[n], v)
                    nc.scalar.activation(stat[:, 2], stat[:, 1], ACT.Sqrt).then_inc(s_std[n], 1)
                    act.wait_ge(s_turn[n], v)
                    if n == 1:
                        for k in range(2):
                            last = nc.scalar.activation(YT[:, 2 * k:2 * k + 2, :], turned(slice(0, C), k), ACT.Copy)
                        last.then_inc(s_yt, 1)
                        break
                    for k in range(2):
                        nc.scalar.activation(XT[0:C, 2 * k:2 * k + 2, 0:T], turned(slice(0, C), k), ACT.Copy)
                        last = nc.scalar.activation(XT[C:128, 2 * k:2 * k + 2, 1:T + 1], turned(slice(C, 128), k), ACT.Copy)
                    last.then_inc(s_xt, 1)
                    act.wait_ge(s_clip, v)
                    nc.scalar.activation(K[:], KC[:], ACT.Exp)
                    for b in range(GRP):
                        last = nc.scalar.activation(ER[:, :, b, :], bank[2 + b][0:HALF, 0:384].rearrange("p (a c) -> p a c", a=2)[:, :, 128:192],
                                                    ACT.Exp, scale=-1.0)
                    last.then_inc(s_exp, 1)
                    act.wait_ge(s_rwt, v)
                    for k in range(2):
                        last = nc.scalar.activation(RWT[:, 2 * k:2 * k + 2, :], turned(slice(0, C), k), ACT.Copy)
                    last.then_inc(s_rwt_sb, 1)

        @block.vector
        def _(dve):
            def norm(n, src, v):
                nc.vector.tensor_reduce(stat[:, 0], src, AX.X, ALU.add)
                dve.drain()
                nc.vector.tensor_scalar(stat[:, 3], stat[:, 0], 1.0 / C, None, ALU.mult)
                dve.drain()
                nc.vector.tensor_tensor(XC[:], src, stat[:, 3].unsqueeze(2).broadcast_to([HALF, 2 * GRP, C]),
                                        ALU.subtract).then_inc(s_cen[n], 1)
                dve.wait_ge(s_sq[n], v)
                nc.vector.tensor_reduce(stat[:, 0], SQ[:], AX.X, ALU.add)
                dve.drain()
                nc.vector.tensor_scalar(stat[:, 1], stat[:, 0], 1.0 / C, EPS, ALU.mult, ALU.add).then_inc(s_var[n], 1)
                dve.wait_ge(s_std[n], v)
                nc.vector.reciprocal(stat[:, 3], stat[:, 2])
                dve.drain()
                for d in range(2):
                    last = nc.vector.tensor_tensor(Y[:].rearrange("p a b d c -> p (a b) d c")[:, :, d, :], XC[:],
                                                   stat[:, 3].unsqueeze(2).broadcast_to([HALF, 2 * GRP, C]), ALU.mult)
                last.then_inc(s_norm[n], 1)

            nc.vector.memset(XT[C:128, :, 0:1], 0.0)
            dve.wait_ge(s_wload, 64)
            nc.vector.tensor_scalar(mixc[C:128, :], mixc[C:128, :], -1.0, 1.0, ALU.mult, ALU.add)
            dve.drain()
            for k in range(3):
                last = nc.vector.tensor_scalar(wmix[:, k, :], wmix[:, k, :], mixc[:, k:k + 1], None, ALU.mult)
            last.then_inc(s_wready, 1)
            with dve.Fori(0, groups) as g:
                v = g + 1
                dve.wait_ge(s_xin, g * 48 + 48)
                norm(0, X[:].rearrange("p a b c -> p (a b) c"), v)
                dve.wait_ge(s_proj, v)
                for b in range(GRP):
                    last = nc.vector.tensor_scalar(KC[:, :, b, :], bank[2 + b][0:HALF, 0:384].rearrange("p (a c) -> p a c", a=2)[:, :, 0:64],
                                                   -60.0, 30.0, ALU.max, ALU.min)
                last.then_inc(s_clip, 1)
                dve.wait_ge(s_exp, v)
                for b in range(GRP):
                    last = nc.vector.tensor_tensor(KV[:, :, b, :], bank[2 + b][0:HALF, 0:384].rearrange("p (a c) -> p a c", a=2)[:, :, 64:128],
                                                   K[:, :, b, :], ALU.mult)
                last.then_inc(s_kv, 1)
                dve.wait_ge(s_mix, v)
                er = ER[:].rearrange("p a b c -> p (a b c)")
                den = DEN[:].rearrange("p g c -> p (g c)")
                nc.vector.scalar_tensor_tensor(out=den, in0=er, scalar=1.0, in1=bank[7][0:HALF, :], op0=ALU.add, op1=ALU.mult)
                dve.drain()
                nc.vector.reciprocal(den, den)
                dve.drain()
                nc.vector.tensor_tensor(RW[:].rearrange("p a b c -> p (a b c)"), bank[6][0:HALF, :], den, ALU.mult).then_inc(s_rw, 1)
                dve.wait_ge(s_ao, v)
                nc.vector.tensor_tensor(H1[:].rearrange("p a b c -> p (a b c)"), bank[2][0:HALF, :],
                                        X[:].rearrange("p a b c -> p (a b c)"), ALU.add).then_inc(s_h1, 1)
                dve.wait_ge(s_h1, v)
                norm(1, H1[:].rearrange("p a b c -> p (a b) c"), v)


def main(nc, ctx, sb, sem, bank, env):
    f32, f16, u32 = env["f32"], env["f16"], env["u32"]
    ALU, ACT, AX = env["ALU"], env["ACT"], env["AX"]
    yT_d, m_d, kv_d, o_d = (env[k] for k in ("yT_d", "m_d", "kv_d", "o_d"))
    ident, ident16, sel_mask, sel_score = (env[k] for k in ("ident", "ident16", "sel_mask", "sel_score"))
    key_of, from_top, causal, s_const = env["key_of"], env["from_top"], env["causal"], env["s_const"]
    table, wq = env["table"], env["wq"]
    passed = env["passed"]
    with ExitStack() as local:
        def sb(name, shape, dt=f32):
            return local.enter_context(nc.sbuf_tensor(name, shape, dt))

        tbl = sb("tbl", [128, CHUNKS, 2 * C])
        pairs = [sb(f"pairs{p}", [128, 2, 2, BLK], f16) for p in range(2)]
        ranks = [sb(f"ranks{p}", [128, BLK], f16) for p in range(2)]
        ex = [sb(f"ex{k}", [128, BLK]) for k in range(AHEAD + 1)]
        wt = [sb(f"wt{k}", [128, BLK]) for k in range(AHEAD + 1)]
        kv_s = sb("kv_s", [2 * C, BLK])
        yt = sb("yt", [C, BLK])
        mh = sb("mh", [C, 2 * NK])
        S = sb("S", [128, TILES, 2, NK])
        S2 = sb("S2", [128, TILES, 2, NK])
        val = sb("val", [128, TILES, 2, TOP])
        idx = sb("idx", [128, TILES, 2, TOP], u32)
        idxf = sb("idxf", [128, TILES, 2, TOP], f16)
        cand = sb("cand", [128, TILES, NCAND])
        cand1 = sb("cand1", [128, TILES, NCAND])
        cand2 = sb("cand2", [128, TILES, NCAND])
        best = sb("best", [128, TILES, TOP])
        picked = sb("picked", [128, TILES, NCAND])
        kept = sb("kept", [128, TILES, TOP], f16)
        below = sb("below", [128, TILES, TOP])
        top_exp = sb("top_exp", [128, TILES, TOP])
        total = sb("total", [128, TILES])
        rtotal = sb("rtotal", [128, TILES])
        rz = [sb(f"rz{p}", [128, BLK]) for p in range(2)]
        sc0 = sb("sc0", [128, TILES, 2, NK])
        sc = sb("sc", [128, TILES, 2, NK])
        sc_hi = sb("sc_hi", [128, TILES, 2 * NK], f16)
        sc_lo = sb("sc_lo", [128, TILES, 2 * NK], f16)
        split = sb("split", [128, 2, BLK], f16)
        is_key = sb("is_key", [128, TILES, 2 * NK, TOP], f16)
        onehot = sb("onehot", [128, TILES, 2 * NK, TOP], f16)
        kT = sb("kT", [C, ATT])
        vT = sb("vT", [C, ATT])
        ya = sb("ya", [C, ATT])
        wqh = sb("wqh", [C, C])
        qT = sb("qT", [C, ATT])
        v_s = sb("v_s", [HALF, 2 * NB, C])
        sim = sb("sim", [HALF, 2 * NB, T])
        prob = sb("prob", [HALF, 2 * NB, T])
        probn = sb("probn", [HALF, 2 * NB, T])
        negmax = sb("negmax", [HALF, 2 * NB])
        psum_ = sb("psum_", [HALF, 2 * NB])
        prec = sb("prec", [HALF, 2 * NB])
        pT = sb("pT", [HALF, NB * 198])
        oT = sb("oT", [C, ATT])

        mask_b = [bank[0], bank[1], bank[5]]
        score_b = [bank[2], bank[3]]
        kv_b = bank[4]
        Bk, Ck = bank[6], bank[7]

        names = ["scores", "probs", "weights", "mixed", "kv_sb",
                 "sims", "sims_sb", "vals", "idxs", "idxf_sb", "cands", "best_v", "firsts", "below", "top_exp", "rtotal", "rz_ps", "rz_sb", "shifted",
                 "hi", "lo", "turned", "split_sb", "ranks_ps", "ranks_sb", "is_key", "oh_one", "oh_two",
                 "q_ps", "q_sb", "v_ps", "v_sb", "negmax", "att_exp", "att_rec", "att_p", "pt0", "pt0_sb",
                 "pt1", "pt1_sb", "pv", "o_sb"]
        s = {n: sem("m_" + n) for n in names}
        s_sim = [sem(f"m_sim{b}") for b in range(NB)]
        s_msk = [sem(f"m_msk{b}") for b in range(NB)]
        d_tbl = [sem(f"d_tbl{k}") for k in range(4)]
        d_sel, d_kv, d_att, d_o = sem("d_sel"), sem("d_kv"), sem("d_att"), sem("d_o")
        d_pairs = [sem(f"d_pairs{p}") for p in range(2)]

        block = local.enter_context(nc.Block())

        def first(n):
            return isinstance(n, int) and n == 0

        @block.sync
        def _(sp):
            def load_table(h, k):
                sp.dma_start(tbl[:, 8 * k:8 * k + 8, :],
                             table[bass.ds(h, 1)].rearrange("o p c d -> (o p) c d")[:, 8 * k:8 * k + 8, :]).then_inc(d_tbl[k], 16)

            def load_selection(n):
                h, blk = n // NBLK, n % NBLK
                sp.dma_start(yt[:], yT_d[:, bass.ds(blk * BLK, BLK)]).then_inc(d_sel, 16)
                sp.dma_start(mh[:], m_d[bass.ds(h, 1)].rearrange("o c k -> (o c) k")).then_inc(d_sel, 16)

            def move_pairs(n, p):
                sp.wait_ge(s["split_sb"], n + 1)
                with nc.allow_non_contiguous_dma(reason="rows of 768 bytes"):
                    for x in range(2):
                        for k in range(2):
                            src = split[64 + 32 * k:96 + 32 * k, x, :]
                            sp.dma_start(pairs[p][32 * x:32 * x + 32, :, k, :],
                                         src.unsqueeze(1).broadcast_to([32, 2, BLK])).then_inc(d_pairs[p], 16)
                            src = split[32 * k:32 * k + 32, x, :]
                            sp.dma_start(pairs[p][64 + 32 * x:96 + 32 * x, k, :, :],
                                         src.unsqueeze(1).broadcast_to([32, 2, BLK])).then_inc(d_pairs[p], 16)

            def load_attention(n):
                m = n - LAG + NBLK
                h, t = m // NBLK, m % NBLK
                col = bass.ds(t * ATT, ATT)
                page = kv_d[bass.ds(h, 1)].rearrange("o c t -> (o c) t")
                sp.dma_start(kT[:], page[0:C, col]).then_inc(d_att, 16)
                sp.dma_start(vT[:], page[C:2 * C, col]).then_inc(d_att, 16)
                sp.dma_start(ya[:], yT_d[:, col]).then_inc(d_att, 16)
                sp.dma_start(wqh[:], wq[bass.ds(h, 1)].rearrange("o c k -> (o c) k")).then_inc(d_att, 16)

            def store_kv(n):
                m = n - 1 + NBLK
                h, blk = m // NBLK, m % NBLK
                sp.wait_ge(s["kv_sb"], n + 1)
                sp.dma_start(kv_d[bass.ds(h, 1)].rearrange("o c t -> (o c) t")[:, bass.ds(blk * BLK, BLK)],
                             kv_s[:]).then_inc(d_kv, 16)

            def store_o(n):
                m = n - LAG + NBLK
                h, t = m // NBLK, m % NBLK
                sp.wait_ge(s["o_sb"], n + 2)
                sp.dma_start(o_d[bass.ds(h, 1)].rearrange("o c t -> (o c) t")[:, bass.ds(t * ATT, ATT)],
                             oT[:]).then_inc(d_o, 16)

            for k in range(4):
                load_table(0, k)
            load_selection(0)
            sp.wait_ge(s["sims"], 1)
            load_selection(1)
            move_pairs(0, 0)
            load_attention(0)
            with sp.Fori(0, HEADS) as h:
                with sp.Fori(0, NBLK // 2) as i:
                    for p in range(2):
                        g = h * NBLK + i * 2 + p
                        store_kv(g)
                        sp.wait_ge(s["sims"], g + 2)
                        load_selection(g + 2)
                        move_pairs(g + 1, 1 - p)
                        sp.wait_ge(s["pv"], g + 1)
                        sp.wait_ge(d_kv, g * 16 + 32)
                        load_attention(g + 1)
                        store_o(g)
                for k in range(4):
                    sp.wait_ge(s["mixed"], h * (4 * NBLK) + (4 * NBLK - 2 + k))
                    load_table((h + 1) % HEADS, k)
            store_kv(STEPS)
            sp.wait_ge(d_kv, 16 * (STEPS + 2))
            for g in range(STEPS, STEPS + LAG):
                sp.wait_ge(s["pv"], g + 1)
                if g + 1 < STEPS + LAG:
                    load_attention(g + 1)
                store_o(g)
            for k in range(4):
                sp.wait_ge(d_tbl[k], 16 * (HEADS + 1))
            sp.wait_ge(d_sel, 32 * (STEPS + 2))
            sp.wait_ge(d_o, 16 * (STEPS + LAG + 1))

        @block.tensor
        def _(pe):
            def select(n, slot):
                if slot == 0:
                    pe.wait_ge(d_sel, n * 32 + 32)
                    for t in range(TILES):
                        last = nc.tensor.matmul(Bk[:, t * 128:t * 128 + 128], yt[:, t * 128:t * 128 + 128], mh[:], start=True, stop=True)
                    last.then_inc(s["sims"], 1)
                if slot == 10:
                    pe.wait_ge(s["lo"], n + 1)
                    if not first(n):
                        pe.wait_ge(s_msk[1], n)
                    a16 = Bk[:].bitcast(f16)
                    for x, src in enumerate((sc_hi, sc_lo)):
                        for t in range(TILES):
                            last = nc.tensor.transpose(a16[:, x * BLK + t * 128:x * BLK + t * 128 + 128], src[:, t, :], ident16[:])
                    last.then_inc(s["turned"], 1)
                if slot == 21:
                    pe.wait_ge(s["rtotal"], n + 1)
                    pe.wait_ge(s["split_sb"], n + 1)
                    for t in range(TILES):
                        last = nc.tensor.matmul(Bk[:, t * 128:t * 128 + 128], rtotal[:, t:t + 1].broadcast_to([128, 128]),
                                                ident[:], start=True, stop=True)
                    last.then_inc(s["rz_ps"], 1)
                if slot in (25, 27, 29):
                    t = (25, 27, 29).index(slot)
                    if t == 0:
                        pe.wait_ge(s["rz_sb"], n + 2)
                    pe.wait_ge(s["oh_two"], n * TILES + (t + 1))
                    pe.wait_ge(s["oh_one"], n * TILES + (t + 1))
                    for a in range(TOP):
                        last = nc.tensor.matmul(Bk[:, t * 128:t * 128 + 128], onehot[:, t, :, a], ident16[:],
                                                start=(a == 0), stop=(a == TOP - 1))
                    if t == TILES - 1:
                        last.then_inc(s["ranks_ps"], 1)

            def attend(n, slot):
                if slot == 2:
                    pe.wait_ge(d_att, n * 64 + 64)
                    hold(pe, s["o_sb"], n + 1, passed["pe"])
                    nc.tensor.matmul(Ck[0:C, 0:ATT], wqh[:], ya[:], start=True, stop=True).then_inc(s["q_ps"], 1)
                if slot == 3:
                    if not isinstance(n, int):
                        hold(pe, s["sims_sb"], n + 2, passed["pe"])
                    for k in range(2 * NB):
                        last = nc.tensor.transpose(Bk[0:HALF, k * C:(k + 1) * C], vT[:, k * HALF:(k + 1) * HALF], ident[0:C, 0:C])
                    last.then_inc(s["v_ps"], 1)
                if slot in (5, 6, 8):
                    b = (5, 6, 8).index(slot)
                    hold(pe, (s["q_sb"], s["v_sb"], s_msk[0])[b], n + 1, passed["pe"])
                    dst = (Ck, Bk, Ck)[b]
                    for a in range(2):
                        last = nc.tensor.matmul(dst[0:HALF, a * T:(a + 1) * T], qT[:, b * T + a * HALF:b * T + a * HALF + HALF],
                                                kT[:, b * T:(b + 1) * T], start=True, stop=True)
                    last.then_inc(s_sim[b], 1)
                if slot in (23, 25):
                    half = (23, 25).index(slot)
                    hold(pe, (s["att_p"], s["pt0_sb"])[half], n + 1, passed["pe"])
                    for b in ((0, 1), (2,))[half]:
                        col = (b % 2) * 198
                        for k, (a, j) in enumerate(((0, 0), (1, 0), (1, 1))):
                            last = nc.tensor.transpose(Ck[0:HALF, col + k * HALF:col + (k + 1) * HALF],
                                                       probn[:, 2 * b + a, j * HALF:(j + 1) * HALF], ident[0:HALF, 0:HALF])
                    last.then_inc(s[("pt0", "pt1")[half]], 1)
                if slot == 28:
                    hold(pe, s["pt1_sb"], n + 1, passed["pe"])
                    for b in range(NB):
                        nc.tensor.matmul(Ck[0:C, b * T:(b + 1) * T], v_s[:, 2 * b, :], pT[:, b * 198:b * 198 + T], start=True, stop=False)
                        last = nc.tensor.matmul(Ck[0:C, b * T + HALF:(b + 1) * T], v_s[:, 2 * b + 1, :],
                                                pT[:, b * 198 + T:b * 198 + 198], start=False, stop=True)
                    last.then_inc(s["pv"], 1)

            def mix(c):
                last = nc.tensor.matmul(kv_b[:, 0:BLK], tbl[:, c, :], wt[c % 4][:], start=(c == 0), stop=(c == CHUNKS - 1))
                if c % 8 == 7:
                    last.then_inc(s["mixed"], 1)

            for slot in range(32):
                select(0, slot)
            pe.wait_ge(d_tbl[3], 16)
            pe.wait_ge(s["weights"], 1)
            nc.tensor.matmul(kv_b[:, 0:BLK], tbl[:, CHUNKS - AHEAD, :], wt[1][:], start=True, stop=False)
            with pe.Fori(0, HEADS) as h:
                with pe.Fori(0, NBLK // 2) as i:
                    for p in range(2):
                        g = h * NBLK + i * 2 + p
                        for c in range(CHUNKS):
                            if c == 0:
                                pe.wait_ge(s["ranks_sb"], g + 1)
                                pe.wait_ge(d_pairs[p], (h * (NBLK // 2) + i) * 128 + 128)
                            pe.wait_ge(s["weights"], g * CHUNKS + (c + (2 if c < 2 else 1)))
                            q = c // 8
                            nc.tensor.matmul(mask_b[c % 3][:, 0:BLK], sel_mask[:, c, :], ranks[p][:], start=True, stop=True)
                            pe.wait_ge(s["probs"], g * CHUNKS + (c + 1))
                            nc.tensor.matmul(score_b[c % 2][:, 0:BLK], sel_score[:, c % 8, :], pairs[p][:, q // 2, q % 2, :],
                                             start=True, stop=True).then_inc(s["scores"], 1)
                            if c == AHEAD:
                                select(g + 1, c)
                                attend(g, c)
                                pe.wait_ge(s["kv_sb"], g + 1)
                            if c % 8 == AHEAD:
                                pe.wait_ge(d_tbl[c // 8], h * 16 + 16)
                            mix((c - AHEAD) % CHUNKS)
                            if c != AHEAD:
                                select(g + 1, c)
                                attend(g, c)
            pe.wait_ge(s["weights"], STEPS * CHUNKS + AHEAD)
            for c in range(CHUNKS - AHEAD, CHUNKS):
                mix(c)
            pe.wait_ge(s["ranks_sb"], STEPS + 1)
            for g in range(STEPS, STEPS + LAG):
                for slot in range(32):
                    attend(g, slot)

        @block.scalar
        def _(act):
            def select(n, slot):
                if slot == 1:
                    act.wait_ge(s["sims"], n + 1)
                    nc.scalar.activation(S[:].rearrange("p t a k -> p (t a k)"), Bk[:, 0:BLK], ACT.Copy).then_inc(s["sims_sb"], 1)
                if slot == 11:
                    act.wait_ge(s["idxs"], n + 1)
                    nc.scalar.activation(idxf[:], idx[:], ACT.Copy).then_inc(s["idxf_sb"], 1)
                if slot == 15:
                    act.wait_ge(s["below"], n + 1)
                    nc.scalar.activation(top_exp[:], below[:], ACT.Exp).then_inc(s["top_exp"], 1)
                if slot == 6:
                    act.wait_ge(s["shifted"], n + 1)
                    nc.scalar.activation(sc_hi[:], sc[:].rearrange("p t a k -> p t (a k)"), ACT.Copy).then_inc(s["hi"], 1)
                if slot == 11:
                    act.wait_ge(s["turned"], n + 1)
                    if not first(n):
                        act.wait_ge(d_pairs[n_parity[0]], moved[0])
                    nc.scalar.activation(split[:].rearrange("p x t -> p (x t)"), Bk[:].bitcast(f16)[:, 0:2 * BLK], ACT.Copy).then_inc(s["split_sb"], 1)
                if slot == 22:
                    act.wait_ge(s["rz_ps"], n + 1)
                    if not first(n):
                        act.wait_ge(s["kv_sb"], n)
                    nc.scalar.activation(rz[n_parity[1]][:], Bk[:, 0:BLK], ACT.Copy).then_inc(s["rz_sb"], 1)
                if slot == 30:
                    act.wait_ge(s["ranks_ps"], n + 1)
                    nc.scalar.activation(ranks[n_parity[1]][:], Bk[:, 0:BLK], ACT.Copy).then_inc(s["ranks_sb"], 1)

            n_parity, moved = [1, 0], [None]

            def attend(n, slot):
                if slot == 3:
                    act.wait_ge(s["q_ps"], n + 1)
                    nc.scalar.activation(qT[:], Ck[0:C, 0:ATT], ACT.Copy, scale=C ** -0.5).then_inc(s["q_sb"], 1)
                if slot == 4:
                    act.wait_ge(s["v_ps"], n + 1)
                    nc.scalar.activation(v_s[:].rearrange("p k c -> p (k c)"), Bk[0:HALF, 0:2 * NB * C], ACT.Copy).then_inc(s["v_sb"], 1)
                if 11 <= slot < 17:
                    k = slot - 11
                    if k % 2 == 0:
                        act.wait_ge(s["negmax"], n * NB + (k // 2 + 1))
                    last = nc.scalar.activation(prob[:, k, :], sim[:, k, :], ACT.Exp, bias=negmax[:, k:k + 1], accum_out=psum_[:, k:k + 1])
                    if k == 5:
                        last.then_inc(s["att_exp"], 1)
                if slot == 24:
                    act.wait_ge(s["pt0"], n + 1)
                    nc.scalar.activation(pT[:, 0:396], Ck[0:HALF, 0:396], ACT.Copy).then_inc(s["pt0_sb"], 1)
                if slot == 26:
                    act.wait_ge(s["pt1"], n + 1)
                    nc.scalar.activation(pT[:, 396:594], Ck[0:HALF, 0:198], ACT.Copy).then_inc(s["pt1_sb"], 1)
                if slot == 29:
                    act.wait_ge(s["pv"], n + 1)
                    act.wait_ge(d_o, n * 16 + 16)
                    nc.scalar.activation(oT[:], Ck[0:C, 0:ATT], ACT.Copy).then_inc(s["o_sb"], 1)

            act.sem_inc(s["o_sb"], 1)
            for k in range(2):
                act.sem_inc(s["probs"], 1)
            act.dma_start(oT[:], yT_d[:, 0:ATT]).then_inc(d_o, 16)
            act.dma_start(kv_s[:], kv_d[0][:, 0:BLK]).then_inc(d_kv, 16)
            for slot in range(32):
                select(0, slot)
            with act.Fori(0, HEADS) as h:
                with act.Fori(0, NBLK // 2) as i:
                    for p in range(2):
                        g = h * NBLK + i * 2 + p
                        n_parity[:] = [p, 1 - p]
                        moved[0] = (h * (NBLK // 2) + i) * 128 + 128
                        for c in range(CHUNKS):
                            act.wait_ge(s["scores"], g * CHUNKS + (c + 1))
                            nc.scalar.activation(ex[c % 4][:], score_b[c % 2][:, 0:BLK], ACT.Exp).then_inc(s["probs"], 1)
                            select(g + 1, c)
                            attend(g, c)
            for g in range(STEPS, STEPS + LAG):
                for slot in range(32):
                    attend(g, slot)

        @block.vector
        def _(dve):
            def select(n, slot):
                if slot in (2, 3):
                    if slot == 2:
                        hold(dve, s["sims_sb"], n + 1, passed["dve"])
                    for t, a in GROUPS[slot - 2]:
                        last = nc.vector.max(val[:, t, a, 0:8], S[:, t, a, :])
                    if slot == 3:
                        last.then_inc(s["firsts"], 1)
                if slot in (4, 5, 6):
                    if slot == 4:
                        dve.drain()
                    for t, a in PARTS[slot - 4]:
                        nc.vector.max_index(idx[:, t, a, 0:8], val[:, t, a, 0:8], S[:, t, a, :])
                        nc.vector.match_replace(S2[:, t, a, :], val[:, t, a, 0:8], S[:, t, a, :], LOWEST)
                if slot in (7, 8):
                    if slot == 7:
                        dve.drain()
                    for t, a in GROUPS[slot - 7]:
                        last = nc.vector.max(val[:, t, a, 8:16], S2[:, t, a, :])
                    if slot == 8:
                        last.then_inc(s["vals"], 1)
                if slot in (9, 10):
                    if slot == 9:
                        dve.drain()
                    for t, a in GROUPS[slot - 9]:
                        last = nc.vector.max_index(idx[:, t, a, 8:16], val[:, t, a, 8:16], S2[:, t, a, :])
                    if slot == 10:
                        last.then_inc(s["idxs"], 1)
                if slot in (11, 13):
                    if slot == 11:
                        hold(dve, s["cands"], n + 1, passed["dve"])
                    else:
                        dve.drain()
                    k = (slot - 11) // 2
                    for t in range(TILES):
                        last = nc.vector.max(best[:, t, 8 * k:8 * k + 8], (cand, cand1)[k][:, t, :])
                    if k == 1:
                        last.then_inc(s["best_v"], 1)
                if slot in (12, 14):
                    dve.drain()
                    k = (slot - 12) // 2
                    for t in range(TILES):
                        nc.vector.match_replace((cand1, cand2)[k][:, t, :], best[:, t, 8 * k:8 * k + 8], (cand, cand1)[k][:, t, :], LOWEST)
                if slot == 15:
                    dve.drain()
                    nc.vector.tensor_tensor(picked[:], cand2[:], cand[:], ALU.not_equal)
                if slot == 16:
                    dve.drain()
                    for a, rows, cols, at in CAND:
                        src = picked[:, :, at:at + rows * cols].rearrange("p t (a b) -> p t a b", a=rows)
                        if cols > 1:
                            with nc.allow_low_precision(reason="counts up to 16"):
                                nc.vector.tensor_reduce(kept[:, :, a:a + rows], src, AX.X, ALU.add)
                        else:
                            nc.vector.tensor_copy(kept[:, :, a:a + rows], picked[:, :, at:at + rows])
                if slot in (16, 17, 18, 19, 20, 21):
                    k = (16, 17, 18, 19, 20, 21).index(slot)
                    if k == 0:
                        dve.wait_ge(s["idxf_sb"], n + 1)
                        if not first(n):
                            dve.wait_ge(s["oh_two"], n * TILES)
                    t, a = k % 3, 1 - k // 3
                    ranked = idxf[:, t, a, :].unsqueeze(1).broadcast_to([128, NK, TOP])
                    nc.vector.tensor_tensor(is_key[:, t, a * NK:(a + 1) * NK, :], key_of[:], ranked, ALU.is_equal).then_inc(s["is_key"], 1)
                if slot in (22, 23, 24):
                    t = slot - 22
                    if t == 0:
                        dve.wait_ge(s["is_key"], n * (2 * TILES) + 2 * TILES)
                        if not first(n):
                            dve.wait_ge(s["ranks_ps"], n)
                    weight = kept[:, t, :].unsqueeze(1).broadcast_to([128, NK, TOP])
                    nc.vector.tensor_tensor(onehot[:, t, 0:NK, :], is_key[:, t, 0:NK, :], weight, ALU.mult).then_inc(s["oh_one"], 1)
                if slot == 17:
                    dve.wait_ge(s["top_exp"], n + 1)
                    nc.vector.tensor_reduce(total[:], top_exp[:], AX.X, ALU.add)
                if slot == 18:
                    dve.drain()
                    nc.vector.reciprocal(rtotal[:], total[:]).then_inc(s["rtotal"], 1)

            def scale_kv(n, p):
                dve.wait_ge(s["rz_sb"], n + 1)
                dve.wait_ge(s["mixed"], n * 4 + 1)
                dve.wait_ge(d_kv, n * 16 + 16)
                nc.vector.tensor_tensor(kv_s[:], kv_b[:, 0:BLK], rz[p][:], ALU.mult).then_inc(s["kv_sb"], 1)

            GROUPS = [[(0, 0), (0, 1), (1, 0)], [(1, 1), (2, 0), (2, 1)]]
            PARTS = [[(0, 0), (0, 1)], [(1, 0), (1, 1)], [(2, 0), (2, 1)]]

            def attend(n, slot):
                if slot in (6, 7, 9):
                    b = (6, 7, 9).index(slot)
                    dve.wait_ge(s_sim[b], n + 1)
                    src = (Ck, Bk, Ck)[b]
                    nc.vector.tensor_tensor(sim[:, 2 * b:2 * b + 2, :].rearrange("p a t -> p (a t)"), src[0:HALF, 0:2 * T],
                                            causal[:].rearrange("p a t -> p (a t)"), ALU.add).then_inc(s_msk[b], 1)
                if slot in (7, 8, 10):
                    b = (7, 8, 10).index(slot)
                    dve.wait_ge(s_msk[b], n + 1)
                    nc.vector.tensor_reduce(negmax[:, 2 * b:2 * b + 2], sim[:, 2 * b:2 * b + 2, :], AX.X, ALU.max, negate=True).then_inc(s["negmax"], 1)
                if slot == 17:
                    dve.wait_ge(s["att_exp"], n + 1)
                    nc.vector.reciprocal(prec[:], psum_[:]).then_inc(s["att_rec"], 1)

            nc.vector.memset(rz[1][:], 0.0).then_inc(s["rz_sb"], 1)
            for k in range(1, AHEAD + 1):
                nc.vector.memset(wt[k][:], 0.0).then_inc(s["weights"], 1)
            for slot in range(32):
                select(0, slot)
            with dve.Fori(0, HEADS) as h:
                with dve.Fori(0, NBLK // 2) as i:
                    for p in range(2):
                        g = h * NBLK + i * 2 + p
                        for c in range(CHUNKS):
                            dve.wait_ge(s["probs"], g * CHUNKS + (c + 3))
                            nc.vector.scalar_tensor_tensor(out=wt[c % 4][:], in0=mask_b[c % 3][:, 0:BLK], scalar=float(TOP), in1=ex[c % 4][:],
                                                           op0=ALU.is_gt, op1=ALU.mult).then_inc(s["weights"], 1)
                            if c == AHEAD - 1:
                                scale_kv(g, 1 - p)
                            select(g + 1, c)
                            attend(g, c)
            scale_kv(STEPS, 1)
            for g in range(STEPS, STEPS + LAG):
                for slot in range(32):
                    attend(g, slot)

        @block.gpsimd
        def _(pool):
            def select(n, slot):
                if slot == 9:
                    pool.wait_ge(s["vals"], n + 1)
                    for a, rows, cols, at in CAND:
                        out = cand[:, :, at:at + rows * cols].rearrange("p t (a b) -> p t a b", a=rows)
                        one = val[:, :, 0, a:a + rows].unsqueeze(3).broadcast_to([128, TILES, rows, cols])
                        two = val[:, :, 1, 0:cols].unsqueeze(2).broadcast_to([128, TILES, rows, cols])
                        last = pool.tensor_tensor(out, one, two, ALU.add)
                    last.then_inc(s["cands"], 1)
                if slot == 4:
                    pool.wait_ge(s["firsts"], n + 1)
                    pool.tensor_tensor(sc0[:], S[:], val[:, :, :, 0:1].broadcast_to([128, TILES, 2, NK]), ALU.subtract)
                    pool.drain()
                    pool.tensor_scalar(sc[:], sc0[:], FLOOR, None, ALU.max).then_inc(s["shifted"], 1)
                if slot == 8:
                    pool.wait_ge(s["hi"], n + 1)
                    pool.tensor_tensor(sc_lo[:], sc[:].rearrange("p t a k -> p t (a k)"), sc_hi[:], ALU.subtract).then_inc(s["lo"], 1)
                if slot == 14:
                    pool.wait_ge(s["best_v"], n + 1)
                    pool.tensor_tensor(below[:], best[:], best[:, :, 0:1].broadcast_to([128, TILES, TOP]), ALU.subtract).then_inc(s["below"], 1)
                if slot in (17, 18, 20):
                    t = (17, 18, 20).index(slot)
                    pool.wait_ge(s["is_key"], n * (2 * TILES) + (t + 1))
                    if t == 0 and not first(n):
                        pool.wait_ge(s["ranks_ps"], n)
                    weight = from_top[:].unsqueeze(1).broadcast_to([128, NK, TOP])
                    pool.tensor_tensor(onehot[:, t, NK:, :], is_key[:, t, NK:, :], weight, ALU.mult).then_inc(s["oh_two"], 1)

            def attend(n, slot):
                if slot == 19:
                    pool.wait_ge(s["att_rec"], n + 1)
                    pool.tensor_tensor(probn[:], prob[:], prec[:].unsqueeze(2).broadcast_to([HALF, 2 * NB, T]), ALU.mult).then_inc(s["att_p"], 1)

            for slot in range(32):
                select(0, slot)
            with pool.Fori(0, STEPS) as g:
                for slot in range(32):
                    select(g + 1, slot)
                    attend(g, slot)
            for g in range(STEPS, STEPS + LAG):
                for slot in range(32):
                    attend(g, slot)


def final(nc, ctx, sb, sem, bank, env):
    f32 = env["f32"]
    ALU = env["ALU"]
    h1_d, o_d, wo, out = env["h1_d"], env["o_d"], env["wo"], env["out"]
    passed = env["passed"]
    with ExitStack() as local:
        def sb(name, shape, dt=f32):
            return local.enter_context(nc.sbuf_tensor(name, shape, dt))

        wo_s = sb("wo_s", [128, 4, C])
        ob = [sb(f"ob{p}", [128, 4, BLK]) for p in range(2)]
        hb = [sb(f"hb{p}", [128, TILES, C]) for p in range(2)]
        res = [sb(f"res{p}", [128, TILES, C]) for p in range(2)]
        f_wo, f_mm, f_res = sem("f_wo"), sem("f_mm"), sem("f_res")
        f_in = [sem(f"f_in{p}") for p in range(2)]
        f_out = [sem(f"f_out{p}") for p in range(2)]
        o_v = o_d[1:HEADS + 1].rearrange("(k e) c t -> (e c) k t", e=2)
        h_v = h1_d.rearrange("(n k p) c -> p n k c", k=TILES, p=128)
        out_v = out.rearrange("b t c -> (b t) c").rearrange("(n k p) c -> p n k c", k=TILES, p=128)
        block = local.enter_context(nc.Block())

        @block.sync
        def _(sp):
            def load(n, p):
                sp.dma_start(ob[p][:], o_v[:, :, bass.ds(n * BLK, BLK)]).then_inc(f_in[p], 16)
                sp.dma_start(hb[p][:], h_v[:, bass.ds(n, 1)].rearrange("p o k c -> p (o k) c")).then_inc(f_in[p], 16)

            def store(n, p):
                sp.dma_start(out_v[:, bass.ds(n, 1)].rearrange("p o k c -> p (o k) c"), res[p][:]).then_inc(f_out[p], 16)

            sp.dma_start(wo_s[:], wo.rearrange("(k p) c -> p k c", p=128)).then_inc(f_wo, 16)
            load(0, 0)
            load(1, 1)
            with sp.Fori(0, NBLK // 2 - 1) as i:
                for p in range(2):
                    sp.wait_ge(f_res, i * 2 + (p + 1))
                    store(i * 2 + p, p)
                    load(i * 2 + (p + 2), p)
            for p in range(2):
                sp.wait_ge(f_res, NBLK - 1 + p)
                store(NBLK - 2 + p, p)
            for p in range(2):
                sp.wait_ge(f_out[p], 16 * (NBLK // 2))

        @block.tensor
        def _(pe):
            pe.wait_ge(f_wo, 16)

            def block_of(n, i, p):
                pe.wait_ge(f_in[p], i * 32 + 32)
                if n is not None:
                    pe.wait_ge(f_res, n)
                for t in range(TILES):
                    for k in range(4):
                        last = nc.tensor.matmul(bank[p][:, t * C:(t + 1) * C], ob[p][:, k, t * 128:(t + 1) * 128],
                                                wo_s[:, k, :], start=(k == 0), stop=(k == 3))
                last.then_inc(f_mm, 1)

            for p in range(2):
                block_of(None, 0, p)
            with pe.Fori(1, NBLK // 2) as i:
                for p in range(2):
                    block_of(i * 2 + (p - 1), i, p)

        @block.vector
        def _(dve):
            def block_of(i, p, again):
                dve.wait_ge(f_mm, i * 2 + (p + 1))
                if again:
                    dve.wait_ge(f_out[p], i * 16)
                nc.vector.tensor_tensor(res[p][:].rearrange("p k c -> p (k c)"), bank[p][:, 0:TILES * C],
                                        hb[p][:].rearrange("p k c -> p (k c)"), ALU.add).then_inc(f_res, 1)

            for p in range(2):
                block_of(0, p, False)
            with dve.Fori(1, NBLK // 2) as i:
                for p in range(2):
                    block_of(i, p, True)


_OUTS = [((B, T, C), "float32")]


def kernel(x, txt, L0_tok_weight, L0_tok_bias, L0_attn_time_w, L0_attn_time_mix_k, L0_attn_time_mix_v,
           L0_attn_time_mix_r, L0_attn_Wk, L0_attn_Wv, L0_attn_Wr, L0_attn_Wo, L0_ffn_Wq_pk, L0_ffn_pk_keys,
           L0_ffn_Wq, L0_ffn_keys_table, L0_ffn_values_table, L0_ffn_Wo):
    import numpy as _np
    import concourse.bacc as _bacc
    from concourse import mybir as _mybir
    from concourse.bass_utils import run_bass_kernel_spmd as _run

    a = _np.asarray
    late = a(L0_attn_time_w)[::-1]
    distance = _np.abs(_np.arange(T)[None, :] - _np.arange(T)[:, None])
    mix = _np.stack([a(m).reshape(C) for m in (L0_attn_time_mix_k, L0_attn_time_mix_v, L0_attn_time_mix_r)], axis=1)
    wkvr = _np.concatenate([a(L0_attn_Wk), a(L0_attn_Wv), a(L0_attn_Wr)], axis=1)

    def rows(tab):
        return a(tab).reshape(HEADS, 2, 32, 2, 8, 4, C).transpose(0, 5, 2, 3, 1, 4, 6).reshape(HEADS, 128, CHUNKS, C)

    wq = a(L0_ffn_Wq).reshape(C, HEADS, C).transpose(1, 0, 2)
    ins = {
        "x": a(x), "txt": a(txt), "tok_w": a(L0_tok_weight), "tok_b": a(L0_tok_bias),
        "toeplitz": late[distance],
        "mix": _np.concatenate([mix, mix], axis=0), "wkvr": _np.concatenate([wkvr, wkvr], axis=0),
        "attn_wo": a(L0_attn_Wo),
        "wqT": a(L0_ffn_Wq_pk).reshape(C, 2, HEADS, DK).transpose(3, 2, 1, 0).reshape(DK, 2 * HEADS, C),
        "keysT": a(L0_ffn_pk_keys).transpose(3, 2, 0, 1).reshape(DK, 2 * HEADS, NK),
        "wq": _np.concatenate([wq[:1], wq], axis=0),
        "table": _np.concatenate([rows(L0_ffn_keys_table), rows(L0_ffn_values_table)], axis=3),
        "wo": a(L0_ffn_Wo),
    }
    nc = _bacc.Bacc("TRN2", target_bir_lowering=False, num_devices=1)
    arrays, args = {}, []
    for name, v in ins.items():
        v = _np.ascontiguousarray(v)
        arrays[f"in_{name}"] = v
        args.append(nc.dram_tensor(f"in_{name}", v.shape, _mybir.dt.from_np(v.dtype), kind="ExternalInput").ap())
    shape, dtype = _OUTS[0]
    args.append(nc.dram_tensor("out_0", shape, _mybir.dt.from_np(_np.dtype(dtype)), kind="ExternalOutput").ap())
    build(nc, *args)
    r = _run(nc, [arrays], core_ids=[0])
    return r.results[0]["out_0"]
```

```python
import numpy as np
import concourse.bass as bass
from concourse import mybir
from contextlib import ExitStack

B, T, C = 64, 132, 64
NIMG, TXT = 4, 128
PH, PW, SW = 64, 25, 12
HALF = T // 2
N = B * T
HEADS, NK, TOP = 8, 64, 16
DK = 32
BLK, TILES = 384, 3
NBLK = N // BLK
NB = 3
ATT = NB * T
NPAD = NBLK * ATT
CHUNKS = NK * NK // 128
GRP = 4
STEPS = HEADS * NBLK
LAG = 3
AHEAD = 3
EPS = 1e-5
LOWEST = -3.4028234663852886e38
FLOOR = -60000.0
CAND = [(0, 1, 16, 0), (1, 3, 8, 16), (4, 4, 4, 40), (8, 8, 1, 56)]
NCAND = 64


def hold(eng, semaphore, value, passed):
    eng.wait_ge(semaphore, value)
    eng.sem_inc(passed, 1)


def build(nc, x, txt, tok_w, tok_b, toeplitz, mix, wkvr, attn_wo, wqT, keysT, wq, table, wo, out):
    f32, f16, u32 = mybir.dt.float32, mybir.dt.float16, mybir.dt.uint32
    ALU, ACT, AX = mybir.AluOpType, mybir.ActivationFunctionType, mybir.AxisListType
    ctx = ExitStack()
    with ctx:
        def sb(name, shape, dt=f32):
            return ctx.enter_context(nc.sbuf_tensor(name, shape, dt))

        def sem(name):
            return ctx.enter_context(nc.semaphore(name))

        bank = [ctx.enter_context(nc.psum_tensor(f"bank{i}", [128, 512], f32)) for i in range(8)]

        h0_d = nc.dram_tensor("h0_d", (B * NIMG, C), f32, kind="Internal").ap()
        h1_d = nc.dram_tensor("h1_d", (N, C), f32, kind="Internal").ap()
        yT_d = nc.dram_tensor("yT_d", (C, NPAD), f32, kind="Internal").ap()
        m_d = nc.dram_tensor("m_d", (HEADS + 1, C, 2 * NK), f32, kind="Internal").ap()
        kv_d = nc.dram_tensor("kv_d", (HEADS + 1, 2 * C, NPAD), f32, kind="Internal").ap()
        o_d = nc.dram_tensor("o_d", (HEADS + 1, C, NPAD), f32, kind="Internal").ap()

        ident = sb("ident", [128, 128])
        ident16 = sb("ident16", [128, 128], f16)
        sel_mask = sb("sel_mask", [128, CHUNKS, 128], f16)
        sel_score = sb("sel_score", [128, 8, 128], f16)
        key_of = sb("key_of", [128, NK, TOP], f16)
        from_top = sb("from_top", [128, TOP], f16)
        causal = sb("causal", [HALF, 2, T])
        s_const = sem("s_const")
        passed = {e: sem("passed_" + e) for e in ("pe", "dve", "sp")}

        front(nc, ctx, sb, sem, bank, locals())
        main(nc, ctx, sb, sem, bank, locals())
        final(nc, ctx, sb, sem, bank, locals())


def front(nc, ctx, sb, sem, bank, env):
    f32, f16 = env["f32"], env["f16"]
    ALU, ACT, AX = env["ALU"], env["ACT"], env["AX"]
    x, txt, out = env["x"], env["txt"], env["out"]
    h0_d, h1_d, yT_d, m_d, kv_d = (env[k] for k in ("h0_d", "h1_d", "yT_d", "m_d", "kv_d"))
    ident, ident16, sel_mask, sel_score = (env[k] for k in ("ident", "ident16", "sel_mask", "sel_score"))
    key_of, from_top, causal, s_const = env["key_of"], env["from_top"], env["causal"], env["s_const"]
    passed = env["passed"]
    with ExitStack() as local:
        def sb(name, shape, dt=f32):
            return local.enter_context(nc.sbuf_tensor(name, shape, dt))

        img = sb("img", [PH, B, C])
        patch_w = sb("patch_w", [PH, PW, C])
        patch_b = sb("patch_b", [C, 1])
        h0T = sb("h0T", [C, B * NIMG])
        h0 = sb("h0", [128, 2, C])
        wmix = sb("wmix", [128, 3, C])
        mixc = sb("mixc", [128, 3])
        wo1 = sb("wo1", [C, C])
        wT = sb("wT", [HALF, 2, T])
        tri = sb("tri", [HALF, 2, T])
        wqT_s = sb("wqT_s", [DK, 2 * HEADS, C])
        keysT_s = sb("keysT_s", [DK, 2 * HEADS, NK])
        m_s = sb("m_s", [C, 2 * HEADS * NK])
        zeros = sb("zeros", [128, NPAD])
        def two(name, shape):
            return [sb(f"{name}{u}", shape) for u in range(2)]

        X = two("X", [HALF, 2, GRP, C])
        XC = two("XC", [HALF, 2 * GRP, C])
        SQ = two("SQ", [HALF, 2 * GRP, C])
        Y = two("Y", [HALF, 2, GRP, 2, C])
        stat = two("stat", [HALF, 4, 2 * GRP])
        XT = two("XT", [128, GRP, T + 1])
        KC = two("KC", [HALF, 2, GRP, C])
        K = two("K", [HALF, 2, GRP, C])
        KV = two("KV", [HALF, 2, GRP, C])
        ER = two("ER", [HALF, 2, GRP, C])
        DEN = two("DEN", [HALF, 2 * GRP, C])
        RW = two("RW", [HALF, 2, GRP, C])
        RWT = two("RWT", [C, GRP, T])
        H1 = two("H1", [HALF, 2, GRP, C])
        YT = two("YT", [C, GRP, T])

        s_img = sem("s_img")
        s_tri = sem("s_tri")
        s_wload = sem("s_wload")
        s_mload = sem("s_mload")
        s_patch, s_gelu, s_h0T, s_h0, s_h0_st = (sem(n) for n in ("s_patch", "s_gelu", "s_h0T", "s_h0", "s_h0_st"))
        s_wready, s_m, s_m_sb, s_m_st, s_zero, s_zero_st = (sem(n) for n in ("s_wready", "s_m", "s_m_sb", "s_m_st", "s_zero", "s_zero_st"))
        def sem2(name):
            return [sem(f"{name}{u}") for u in range(2)]

        s_cen, s_sq, s_var, s_std, s_norm, s_turn = (
            [sem2(f"{n}{k}_") for k in range(2)] for n in ("s_cen", "s_sq", "s_var", "s_std", "s_norm", "s_turn"))
        s_xin, s_xt, s_proj, s_clip, s_exp, s_kv, s_mix, s_rw, s_rwt, s_rwt_sb, s_ao, s_h1, s_h1_st, s_yt, s_yt_st = (
            sem2(n) for n in ("s_xin", "s_xt", "s_proj", "s_clip", "s_exp", "s_kv", "s_mix", "s_rw", "s_rwt",
                              "s_rwt_sb", "s_ao", "s_h1", "s_h1_st", "s_yt", "s_yt_st"))

        steps = B // (2 * GRP)
        both = range(2)

        def turned(u, rows, k, b):
            return bank[4 * u + k + b][rows, 0:2 * T].rearrange("p (b t) -> p b t", b=2)

        def four(u, k):
            return bank[4 * u + k][0:HALF, :].rearrange("p (a b c) -> p a b c", a=2, b=GRP)

        block = local.enter_context(nc.Block())

        @block.sync
        def _(sp):
            with nc.allow_non_contiguous_dma(reason="rows of 256 bytes"):
                sp.dma_start(img[:], x.rearrange("b c h w -> h (b c) w")).then_inc(s_img, 16)
                sp.dma_start(patch_w[:], env["tok_w"].rearrange("(h w) d -> h w d", h=PH)).then_inc(s_img, 16)
                sp.dma_start(patch_b[:], env["tok_b"].rearrange("(d o) -> d o", o=1)).then_inc(s_img, 16)
                sp.dma_start(wmix[:].rearrange("p a b -> p (a b)"), env["wkvr"]).then_inc(s_wload, 16)
                sp.dma_start(mixc[:], env["mix"]).then_inc(s_wload, 16)
                sp.dma_start(wo1[:], env["attn_wo"]).then_inc(s_wload, 16)
                sp.dma_start(wT[:], env["toeplitz"].rearrange("(a u) t -> u a t", a=2)).then_inc(s_wload, 16)
                sp.dma_start(wqT_s[:], env["wqT"]).then_inc(s_mload, 16)
                sp.dma_start(keysT_s[:], env["keysT"]).then_inc(s_mload, 16)
                sp.wait_ge(s_h0, 1)
                sp.dma_start(h0_d.rearrange("(k p) d -> p k d", k=2), h0[:]).then_inc(s_h0_st, 16)
                sp.wait_ge(s_h0_st, 16)
                h0_v = h0_d.rearrange("(b n) d -> n b d", n=NIMG)
                txt_v = txt.rearrange("b t d -> t b d")
                h1_v = h1_d.rearrange("(b a t) d -> t a b d", a=2, t=HALF)
                yT_v = yT_d[:, 0:N].rearrange("c (b t) -> c b t", t=T)

                def load(g, u):
                    b = bass.ds(g * (2 * GRP) + u * GRP, GRP)
                    sp.dma_start(X[u][0:NIMG, 0], h0_v[:, b, :]).then_inc(s_xin[u], 16)
                    sp.dma_start(X[u][NIMG:HALF, 0], txt_v[0:HALF - NIMG, b, :]).then_inc(s_xin[u], 16)
                    sp.dma_start(X[u][:, 1], txt_v[HALF - NIMG:TXT, b, :]).then_inc(s_xin[u], 16)

                for u in both:
                    load(0, u)
                sp.wait_ge(s_zero, 1)
                sp.dma_start(kv_d[0], zeros[:]).then_inc(s_zero_st, 16)
                for h in range(1, HEADS + 1):
                    sp.dma_start(kv_d[h][:, N:NPAD], zeros[:, 0:NPAD - N]).then_inc(s_zero_st, 16)
                sp.dma_start(yT_d[:, N:NPAD], zeros[0:C, 0:NPAD - N]).then_inc(s_zero_st, 16)
                sp.wait_ge(s_m_sb, 1)
                for h in range(HEADS + 1):
                    sp.dma_start(m_d[h], m_s[:, 128 * (h % HEADS):128 * (h % HEADS) + 128]).then_inc(s_m_st, 16)
                for u in both:
                    sp.dma_start(YT[u][:].rearrange("c b t -> c (b t)"), zeros[0:C, 0:GRP * T]).then_inc(s_yt_st[u], 16)
                with sp.Fori(0, steps) as g:
                    for u in both:
                        b = bass.ds(g * (2 * GRP) + u * GRP, GRP)
                        sp.wait_ge(s_h1[u], g + 1)
                        for a in range(2):
                            sp.dma_start(h1_v[:, a, b, :], H1[u][:, a]).then_inc(s_h1_st[u], 16)
                    for u in both:
                        sp.wait_ge(s_h1_st[u], g * 32 + 32)
                        load((g + 1) % steps, u)
                    for u in both:
                        b = bass.ds(g * (2 * GRP) + u * GRP, GRP)
                        sp.wait_ge(s_yt[u], g + 1)
                        sp.dma_start(yT_v[:, b, :], YT[u][:]).then_inc(s_yt_st[u], 16)
                for u in both:
                    sp.wait_ge(s_xin[u], 48 * (steps + 1))
                    sp.wait_ge(s_yt_st[u], 16 * (steps + 1))
                sp.wait_ge(s_zero_st, 16 * (HEADS + 2))
                sp.wait_ge(s_m_st, 16 * (HEADS + 1))

        @block.gpsimd
        def _(pool):
            pool.memset(ident[:], 0.0)
            pool.memset(ident16[:], 0.0)
            pool.memset(tri[:], 1.0)
            pool.memset(causal[:], 0.0)
            pool.drain()

            def one_where_zero(tile, pattern, base):
                pool.affine_select(out=tile, in_=tile, compare_op=ALU.not_equal, fill=1.0, base=base,
                                   pattern=pattern, channel_multiplier=1)

            one_where_zero(ident[:], [[-1, 128]], 0)
            one_where_zero(ident16[:], [[-1, 128]], 0)
            pool.drain().then_inc(s_const, 1)
            pool.wait_ge(s_wload, 64)
            for a in range(2):
                for w in (tri, wT):
                    pool.affine_select(out=w[:, a, :], in_=w[:, a, :], compare_op=ALU.is_ge, fill=0.0,
                                       base=-HALF * a, pattern=[[1, T]], channel_multiplier=-1)
                pool.affine_select(out=causal[:, a, :], in_=causal[:, a, :], compare_op=ALU.is_ge, fill=LOWEST,
                                   base=HALF * a, pattern=[[-1, T]], channel_multiplier=1)
            pool.drain().then_inc(s_tri, 1)
            pool.memset(sel_mask[:], 0.0)
            pool.memset(sel_score[:], 0.0)
            pool.iota(key_of[:], [[1, NK], [0, TOP]], base=0, channel_multiplier=0, allow_small_or_imprecise_dtypes=True)
            pool.iota(from_top[:], [[-1, TOP]], base=TOP, channel_multiplier=0, allow_small_or_imprecise_dtypes=True)
            pool.drain()
            sm = sel_mask[:].rearrange("r (q c) (a b) -> r q c a b", q=4, a=4)
            for q in range(4):
                one_where_zero(sm[:, q], [[-4, 8], [-1, 4], [0, 32]], -32 * (q // 2))
            ss = sel_score[:].rearrange("r c (a b) -> r c a b", a=4)
            pool.drain()
            for q in range(4):
                one_where_zero(sm[:, q], [[0, 8], [0, 4], [-1, 32]], -64 - 32 * (q % 2))
            for k in range(2):
                one_where_zero(ss, [[0, 8], [0, 4], [-1, 32]], -32 * k)
                pool.drain()
                one_where_zero(ss, [[-4, 8], [-1, 4], [0, 32]], -64 - 32 * k)
                pool.drain()
            pool.drain()

        @block.tensor
        def _(pe):
            pe.wait_ge(s_img, 48)
            for w in range(PW):
                last = nc.tensor.matmul(bank[0][0:C, 0:B * NIMG].rearrange("d (b n) -> d b n", n=NIMG),
                                        patch_w[:, w, :], img[:, :, w:w + SW * (NIMG - 1) + 1:SW],
                                        start=(w == 0), stop=(w == PW - 1))
            last.then_inc(s_patch, 1)
            pe.wait_ge(s_mload, 32)
            for k in range(2 * HEADS):
                last = nc.tensor.matmul(bank[2 + k // 8][0:C, (k % 8) * NK:(k % 8) * NK + NK],
                                        wqT_s[:, k, :], keysT_s[:, k, :], start=True, stop=True)
            last.then_inc(s_m, 1)
            pe.wait_ge(s_const, 1)
            pe.wait_ge(s_gelu, 1)
            for k in range(2):
                last = nc.tensor.transpose(bank[1][:, k * C:(k + 1) * C], h0T[:, k * 128:(k + 1) * 128], ident[0:C, 0:C])
            last.then_inc(s_h0T, 1)
            pe.wait_ge(s_wready, 1)
            pe.wait_ge(s_tri, 1)
            pe.wait_ge(s_m_sb, 1)
            pe.wait_ge(s_h0, 1)
            for u in both:
                pe.sem_inc(s_turn[1][u], 1)

            def turn(u, k, rows, source):
                for b in range(GRP):
                    for a in range(2):
                        last = nc.tensor.transpose(turned(u, rows, k, b // 2)[:, b % 2, a * HALF:(a + 1) * HALF],
                                                   source(a, b), ident[0:HALF, 0:HALF])
                return last

            with pe.Fori(0, steps) as g:
                v = g + 1
                for u in both:
                    hold(pe, s_norm[0][u], v, passed["pe"])
                    turn(u, 0, slice(0, 128), lambda a, b: Y[u][:, a, b].rearrange("p d c -> p (d c)")).then_inc(s_turn[0][u], 1)
                for u in both:
                    pe.wait_ge(s_xt[u], v)
                    for k in range(3):
                        for b in range(GRP):
                            for a in range(2):
                                last = nc.tensor.matmul(four(u, 1 + k)[:, a, b, :], XT[u][:, b, a * HALF:(a + 1) * HALF],
                                                        wmix[:, k, :], start=True, stop=True)
                    last.then_inc(s_proj[u], 1)
                for u in both:
                    pe.wait_ge(s_kv[u], v)
                    for w, src, k in ((wT, KV, 0), (tri, K, 1)):
                        dst = bank[4 * u + k][0:HALF, :]
                        rows = [src[u][:, e].rearrange("p b c -> p (b c)") for e in range(2)]
                        nc.tensor.matmul(dst[:, 0:256], w[:, 0, 0:HALF], rows[0], start=True, stop=True)
                        nc.tensor.matmul(dst[:, 256:512], w[:, 0, HALF:T], rows[0], start=True, stop=False)
                        last = nc.tensor.matmul(dst[:, 256:512], w[:, 1, HALF:T], rows[1], start=False, stop=True)
                    last.then_inc(s_mix[u], 1)
                for u in both:
                    hold(pe, s_rw[u], v, passed["pe"])
                    turn(u, 2, slice(0, C), lambda a, b: RW[u][:, a, b]).then_inc(s_rwt[u], 1)
                for u in both:
                    hold(pe, s_rwt_sb[u], v, passed["pe"])
                    for b in range(GRP):
                        for a in range(2):
                            last = nc.tensor.matmul(four(u, 0)[:, a, b, :], RWT[u][:, b, a * HALF:(a + 1) * HALF],
                                                    wo1[:], start=True, stop=True)
                    last.then_inc(s_ao[u], 1)
                for u in both:
                    hold(pe, s_norm[1][u], v, passed["pe"])
                    turn(u, 2, slice(0, C), lambda a, b: Y[u][:, a, b, 0]).then_inc(s_turn[1][u], 1)

        @block.scalar
        def _(act):
            act.wait_ge(s_patch, 1)
            nc.scalar.activation(h0T[:], bank[0][0:C, 0:B * NIMG], ACT.Gelu, bias=patch_b[:, 0:1]).then_inc(s_gelu, 1)
            act.wait_ge(s_m, 1)
            nc.scalar.activation(m_s[:, 0:512], bank[2][0:C, :], ACT.Copy)
            nc.scalar.activation(m_s[:, 512:1024], bank[3][0:C, :], ACT.Copy).then_inc(s_m_sb, 1)
            act.wait_ge(s_h0T, 1)
            nc.scalar.activation(h0[:].rearrange("p k c -> p (k c)"), bank[1][:, 0:128], ACT.Copy).then_inc(s_h0, 1)
            act.wait_ge(s_wready, 1)

            def norm(n, v):
                for u in both:
                    act.wait_ge(s_cen[n][u], v)
                    nc.scalar.activation(SQ[u][:], XC[u][:], ACT.Square).then_inc(s_sq[n][u], 1)
                for u in both:
                    act.wait_ge(s_var[n][u], v)
                    nc.scalar.activation(stat[u][:, 2], stat[u][:, 1], ACT.Sqrt).then_inc(s_std[n][u], 1)

            with act.Fori(0, steps) as g:
                v = g + 1
                norm(0, v)
                for u in both:
                    act.wait_ge(s_turn[0][u], v)
                    for k in range(2):
                        nc.scalar.activation(XT[u][0:C, 2 * k:2 * k + 2, 0:T], turned(u, slice(0, C), 0, k), ACT.Copy)
                        last = nc.scalar.activation(XT[u][C:128, 2 * k:2 * k + 2, 1:T + 1], turned(u, slice(C, 128), 0, k), ACT.Copy)
                    last.then_inc(s_xt[u], 1)
                for u in both:
                    act.wait_ge(s_clip[u], v)
                    nc.scalar.activation(K[u][:], KC[u][:], ACT.Exp)
                    nc.scalar.activation(ER[u][:].rearrange("p a b c -> p (a b c)"), bank[4 * u + 3][0:HALF, :], ACT.Exp,
                                         scale=-1.0).then_inc(s_exp[u], 1)
                for u in both:
                    act.wait_ge(s_rwt[u], v)
                    for k in range(2):
                        last = nc.scalar.activation(RWT[u][:, 2 * k:2 * k + 2, :], turned(u, slice(0, C), 2, k), ACT.Copy)
                    last.then_inc(s_rwt_sb[u], 1)
                norm(1, v)
                for u in both:
                    act.wait_ge(s_turn[1][u], v + 1)
                    act.wait_ge(s_yt_st[u], g * 16 + 16)
                    for k in range(2):
                        last = nc.scalar.activation(YT[u][:, 2 * k:2 * k + 2, :], turned(u, slice(0, C), 2, k), ACT.Copy)
                    last.then_inc(s_yt[u], 1)

        @block.vector
        def _(dve):
            def norm(n, source, v):
                wide = [HALF, 2 * GRP, C]
                for u in both:
                    nc.vector.tensor_reduce(stat[u][:, 0], source(u), AX.X, ALU.add)
                dve.drain()
                for u in both:
                    nc.vector.tensor_scalar(stat[u][:, 3], stat[u][:, 0], 1.0 / C, None, ALU.mult)
                dve.drain()
                for u in both:
                    nc.vector.tensor_tensor(XC[u][:], source(u), stat[u][:, 3].unsqueeze(2).broadcast_to(wide),
                                            ALU.subtract).then_inc(s_cen[n][u], 1)
                for u in both:
                    dve.wait_ge(s_sq[n][u], v)
                    nc.vector.tensor_reduce(stat[u][:, 0], SQ[u][:], AX.X, ALU.add)
                    dve.drain()
                    nc.vector.tensor_scalar(stat[u][:, 1], stat[u][:, 0], 1.0 / C, EPS, ALU.mult, ALU.add).then_inc(s_var[n][u], 1)
                for u in both:
                    dve.wait_ge(s_std[n][u], v)
                    nc.vector.reciprocal(stat[u][:, 3], stat[u][:, 2])
                    dve.drain()
                    if n == 0:
                        dve.wait_ge(s_turn[1][u], v)
                    for d in range(2 - n):
                        last = nc.vector.tensor_tensor(Y[u][:].rearrange("p a b d c -> p (a b) d c")[:, :, d, :], XC[u][:],
                                                       stat[u][:, 3].unsqueeze(2).broadcast_to(wide), ALU.mult)
                    last.then_inc(s_norm[n][u], 1)

            nc.vector.memset(zeros[:], 0.0).then_inc(s_zero, 1)
            for u in both:
                nc.vector.memset(XT[u][C:128, :, 0:1], 0.0)
            dve.wait_ge(s_wload, 64)
            nc.vector.tensor_scalar(mixc[C:128, :], mixc[C:128, :], -1.0, 1.0, ALU.mult, ALU.add)
            dve.drain()
            for k in range(3):
                last = nc.vector.tensor_scalar(wmix[:, k, :], wmix[:, k, :], mixc[:, k:k + 1], None, ALU.mult)
            last.then_inc(s_wready, 1)
            with dve.Fori(0, steps) as g:
                v = g + 1
                for u in both:
                    dve.wait_ge(s_xin[u], g * 48 + 48)
                norm(0, lambda u: X[u][:].rearrange("p a b c -> p (a b) c"), v)
                for u in both:
                    dve.wait_ge(s_proj[u], v)
                    nc.vector.tensor_scalar(KC[u][:].rearrange("p a b c -> p (a b c)"), bank[4 * u + 1][0:HALF, :],
                                            -60.0, 30.0, ALU.max, ALU.min).then_inc(s_clip[u], 1)
                for u in both:
                    dve.wait_ge(s_exp[u], v)
                    nc.vector.tensor_tensor(KV[u][:].rearrange("p a b c -> p (a b c)"), bank[4 * u + 2][0:HALF, :],
                                            K[u][:].rearrange("p a b c -> p (a b c)"), ALU.mult).then_inc(s_kv[u], 1)
                for u in both:
                    dve.wait_ge(s_mix[u], v)
                    er = ER[u][:].rearrange("p a b c -> p (a b c)")
                    den = DEN[u][:].rearrange("p g c -> p (g c)")
                    nc.vector.scalar_tensor_tensor(out=den, in0=er, scalar=1.0, in1=bank[4 * u + 1][0:HALF, :], op0=ALU.add, op1=ALU.mult)
                    dve.drain()
                    nc.vector.reciprocal(den, den)
                    dve.drain()
                    nc.vector.tensor_tensor(RW[u][:].rearrange("p a b c -> p (a b c)"), bank[4 * u][0:HALF, :], den,
                                            ALU.mult).then_inc(s_rw[u], 1)
                for u in both:
                    dve.wait_ge(s_ao[u], v)
                    nc.vector.tensor_tensor(H1[u][:].rearrange("p a b c -> p (a b c)"), bank[4 * u][0:HALF, :],
                                            X[u][:].rearrange("p a b c -> p (a b c)"), ALU.add).then_inc(s_h1[u], 1)
                dve.drain()
                norm(1, lambda u: H1[u][:].rearrange("p a b c -> p (a b) c"), v)


def main(nc, ctx, sb, sem, bank, env):
    f32, f16, u32 = env["f32"], env["f16"], env["u32"]
    ALU, ACT, AX = env["ALU"], env["ACT"], env["AX"]
    yT_d, m_d, kv_d, o_d = (env[k] for k in ("yT_d", "m_d", "kv_d", "o_d"))
    ident, ident16, sel_mask, sel_score = (env[k] for k in ("ident", "ident16", "sel_mask", "sel_score"))
    key_of, from_top, causal, s_const = env["key_of"], env["from_top"], env["causal"], env["s_const"]
    table, wq = env["table"], env["wq"]
    passed = env["passed"]
    with ExitStack() as local:
        def sb(name, shape, dt=f32):
            return local.enter_context(nc.sbuf_tensor(name, shape, dt))

        tbl = sb("tbl", [128, CHUNKS, 2 * C])
        pairs = [sb(f"pairs{p}", [128, 2, 2, BLK], f16) for p in range(2)]
        ranks = [sb(f"ranks{p}", [128, BLK], f16) for p in range(2)]
        ex = [sb(f"ex{k}", [128, BLK]) for k in range(AHEAD + 1)]
        wt = [sb(f"wt{k}", [128, BLK]) for k in range(AHEAD + 1)]
        kv_s = sb("kv_s", [2 * C, BLK])
        yt = sb("yt", [C, BLK])
        mh = sb("mh", [C, 2 * NK])
        S = sb("S", [128, TILES, 2, NK])
        S2 = sb("S2", [128, TILES, 2, NK])
        val = sb("val", [128, TILES, 2, TOP])
        idx = sb("idx", [128, TILES, 2, TOP], u32)
        idxf = sb("idxf", [128, TILES, 2, TOP], f16)
        cand = sb("cand", [128, TILES, NCAND])
        cand1 = sb("cand1", [128, TILES, NCAND])
        cand2 = sb("cand2", [128, TILES, NCAND])
        best = sb("best", [128, TILES, TOP])
        picked = sb("picked", [128, TILES, NCAND])
        kept = sb("kept", [128, TILES, TOP], f16)
        below = sb("below", [128, TILES, TOP])
        top_exp = sb("top_exp", [128, TILES, TOP])
        total = sb("total", [128, TILES])
        rtotal = sb("rtotal", [128, TILES])
        rz = [sb(f"rz{p}", [128, BLK]) for p in range(2)]
        sc0 = sb("sc0", [128, TILES, 2, NK])
        sc = sb("sc", [128, TILES, 2, NK])
        sc_hi = sb("sc_hi", [128, TILES, 2 * NK], f16)
        sc_lo = sb("sc_lo", [128, TILES, 2 * NK], f16)
        split = sb("split", [128, 2, BLK], f16)
        is_key = sb("is_key", [128, TILES, 2 * NK, TOP], f16)
        onehot = sb("onehot", [128, TILES, 2 * NK, TOP], f16)
        oh_half = sb("oh_half", [128, TILES, 2 * NK, TOP // 2], f16)
        oh_quarter = sb("oh_quarter", [128, TILES, 2 * NK, TOP // 4], f16)
        kT = sb("kT", [C, ATT])
        vT = sb("vT", [C, ATT])
        ya = sb("ya", [C, ATT])
        wqh = sb("wqh", [C, C])
        qT = sb("qT", [C, ATT])
        v_s = sb("v_s", [HALF, 2 * NB, C])
        sim = sb("sim", [HALF, 2 * NB, T])
        prob = sb("prob", [HALF, 2 * NB, T])
        probn = sb("probn", [HALF, 2 * NB, T])
        negmax = sb("negmax", [HALF, 2 * NB])
        psum_ = sb("psum_", [HALF, 2 * NB])
        prec = sb("prec", [HALF, 2 * NB])
        pT = sb("pT", [HALF, NB * 198])
        oT = sb("oT", [C, ATT])

        mask_b = [bank[0], bank[1], bank[5]]
        score_b = [bank[2], bank[3]]
        kv_b = bank[4]
        Bk, Ck = bank[6], bank[7]

        names = ["scores", "probs", "weights", "mixed", "kv_sb",
                 "sims", "sims_sb", "vals", "idxs", "idxf_sb", "cands", "best_v", "firsts", "below", "top_exp", "rtotal", "rz_ps", "rz_sb", "shifted",
                 "hi", "lo", "turned", "split_sb", "ranks_ps", "ranks_sb", "is_key", "oh_one", "oh_two", "halved", "quartered",
                 "q_ps", "q_sb", "v_ps", "v_sb", "negmax", "att_exp", "att_rec", "att_p", "pt0", "pt0_sb",
                 "pt1", "pt1_sb", "pv", "o_sb"]
        s = {n: sem("m_" + n) for n in names}
        s_sim = [sem(f"m_sim{b}") for b in range(NB)]
        s_msk = [sem(f"m_msk{b}") for b in range(NB)]
        d_tbl = [sem(f"d_tbl{k}") for k in range(4)]
        d_sel, d_kv, d_att, d_o = sem("d_sel"), sem("d_kv"), sem("d_att"), sem("d_o")
        d_pairs = [sem(f"d_pairs{p}") for p in range(2)]

        block = local.enter_context(nc.Block())

        def first(n):
            return isinstance(n, int) and n == 0

        @block.sync
        def _(sp):
            def load_table(h, k):
                sp.dma_start(tbl[:, 8 * k:8 * k + 8, :],
                             table[bass.ds(h, 1)].rearrange("o p c d -> (o p) c d")[:, 8 * k:8 * k + 8, :]).then_inc(d_tbl[k], 16)

            def load_selection(n):
                h, blk = n // NBLK, n % NBLK
                sp.dma_start(yt[:], yT_d[:, bass.ds(blk * BLK, BLK)]).then_inc(d_sel, 16)
                sp.dma_start(mh[:], m_d[bass.ds(h, 1)].rearrange("o c k -> (o c) k")).then_inc(d_sel, 16)

            def move_pairs(n, p):
                sp.wait_ge(s["split_sb"], n + 1)
                with nc.allow_non_contiguous_dma(reason="rows of 768 bytes"):
                    for x in range(2):
                        for k in range(2):
                            src = split[64 + 32 * k:96 + 32 * k, x, :]
                            sp.dma_start(pairs[p][32 * x:32 * x + 32, :, k, :],
                                         src.unsqueeze(1).broadcast_to([32, 2, BLK])).then_inc(d_pairs[p], 16)
                            src = split[32 * k:32 * k + 32, x, :]
                            sp.dma_start(pairs[p][64 + 32 * x:96 + 32 * x, k, :, :],
                                         src.unsqueeze(1).broadcast_to([32, 2, BLK])).then_inc(d_pairs[p], 16)

            def load_attention(n):
                m = n - LAG + NBLK
                h, t = m // NBLK, m % NBLK
                col = bass.ds(t * ATT, ATT)
                page = kv_d[bass.ds(h, 1)].rearrange("o c t -> (o c) t")
                sp.dma_start(kT[:], page[0:C, col]).then_inc(d_att, 16)
                sp.dma_start(vT[:], page[C:2 * C, col]).then_inc(d_att, 16)
                sp.dma_start(ya[:], yT_d[:, col]).then_inc(d_att, 16)
                sp.dma_start(wqh[:], wq[bass.ds(h, 1)].rearrange("o c k -> (o c) k")).then_inc(d_att, 16)

            def store_kv(n):
                m = n - 1 + NBLK
                h, blk = m // NBLK, m % NBLK
                sp.wait_ge(s["kv_sb"], n + 1)
                sp.dma_start(kv_d[bass.ds(h, 1)].rearrange("o c t -> (o c) t")[:, bass.ds(blk * BLK, BLK)],
                             kv_s[:]).then_inc(d_kv, 16)

            def store_o(n):
                m = n - LAG + NBLK
                h, t = m // NBLK, m % NBLK
                sp.wait_ge(s["o_sb"], n + 2)
                sp.dma_start(o_d[bass.ds(h, 1)].rearrange("o c t -> (o c) t")[:, bass.ds(t * ATT, ATT)],
                             oT[:]).then_inc(d_o, 16)

            for k in range(4):
                load_table(0, k)
            load_selection(0)
            sp.wait_ge(s["sims"], 1)
            load_selection(1)
            move_pairs(0, 0)
            load_attention(0)
            with sp.Fori(0, HEADS) as h:
                with sp.Fori(0, NBLK // 2) as i:
                    for p in range(2):
                        g = h * NBLK + i * 2 + p
                        store_kv(g)
                        sp.wait_ge(s["sims"], g + 2)
                        load_selection(g + 2)
                        move_pairs(g + 1, 1 - p)
                        sp.wait_ge(s["pv"], g + 1)
                        sp.wait_ge(d_kv, g * 16 + 32)
                        load_attention(g + 1)
                        store_o(g)
                for k in range(4):
                    sp.wait_ge(s["mixed"], h * (4 * NBLK) + (4 * NBLK - 2 + k))
                    load_table((h + 1) % HEADS, k)
            store_kv(STEPS)
            sp.wait_ge(d_kv, 16 * (STEPS + 2))
            for g in range(STEPS, STEPS + LAG):
                sp.wait_ge(s["pv"], g + 1)
                if g + 1 < STEPS + LAG:
                    load_attention(g + 1)
                store_o(g)
            for k in range(4):
                sp.wait_ge(d_tbl[k], 16 * (HEADS + 1))
            sp.wait_ge(d_sel, 32 * (STEPS + 2))
            sp.wait_ge(d_o, 16 * (STEPS + LAG + 1))

        @block.tensor
        def _(pe):
            def side_scores(n):
                pe.wait_ge(d_sel, n * 32 + 32)
                if not first(n):
                    pe.wait_ge(s["o_sb"], n)
                for t in range(TILES):
                    last = nc.tensor.matmul(Ck[:, t * 128:t * 128 + 128], yt[:, t * 128:t * 128 + 128], mh[:], start=True, stop=True)
                last.then_inc(s["sims"], 1)

            def select(n, slot):
                if slot == 31:
                    side_scores(n + 1)
                if slot == 10:
                    pe.wait_ge(s["lo"], n + 1)
                    if not first(n):
                        pe.wait_ge(s_msk[1], n)
                    a16 = Bk[:].bitcast(f16)
                    for x, src in enumerate((sc_hi, sc_lo)):
                        for t in range(TILES):
                            last = nc.tensor.transpose(a16[:, x * BLK + t * 128:x * BLK + t * 128 + 128], src[:, t, :], ident16[:])
                    last.then_inc(s["turned"], 1)
                if slot == 20:
                    pe.wait_ge(s["rtotal"], n + 1)
                    pe.wait_ge(s["split_sb"], n + 1)
                    for t in range(TILES):
                        last = nc.tensor.matmul(Bk[:, t * 128:t * 128 + 128], rtotal[:, t:t + 1].broadcast_to([128, 128]),
                                                ident[:], start=True, stop=True)
                    last.then_inc(s["rz_ps"], 1)
                for t in {28: (0,), 29: (1, 2)}.get(slot, ()):
                    if t == 0:
                        pe.wait_ge(s["rz_sb"], n + 2)
                    pe.wait_ge(s["quartered"], n * TILES + (t + 1))
                    for a in range(TOP // 4):
                        last = nc.tensor.matmul(Bk[:, t * 128:t * 128 + 128], oh_quarter[:, t, :, a], ident16[:],
                                                start=(a == 0), stop=(a == TOP // 4 - 1))
                    if t == TILES - 1:
                        last.then_inc(s["ranks_ps"], 1)

            def attend(n, slot):
                if slot == 2:
                    pe.wait_ge(d_att, n * 64 + 64)
                    pe.wait_ge(s["sims_sb"], min(n + 2, STEPS + 2) if isinstance(n, int) else n + 2)
                    hold(pe, s["o_sb"], n + 1, passed["pe"])
                    nc.tensor.matmul(Ck[0:C, 0:ATT], wqh[:], ya[:], start=True, stop=True).then_inc(s["q_ps"], 1)
                if slot == 3:
                    for k in range(2 * NB):
                        last = nc.tensor.transpose(Bk[0:HALF, k * C:(k + 1) * C], vT[:, k * HALF:(k + 1) * HALF], ident[0:C, 0:C])
                    last.then_inc(s["v_ps"], 1)
                if slot in (5, 6, 8):
                    b = (5, 6, 8).index(slot)
                    hold(pe, (s["q_sb"], s["v_sb"], s_msk[0])[b], n + 1, passed["pe"])
                    dst = (Ck, Bk, Ck)[b]
                    for a in range(2):
                        last = nc.tensor.matmul(dst[0:HALF, a * T:(a + 1) * T], qT[:, b * T + a * HALF:b * T + a * HALF + HALF],
                                                kT[:, b * T:(b + 1) * T], start=True, stop=True)
                    last.then_inc(s_sim[b], 1)
                if slot in (23, 25):
                    half = (23, 25).index(slot)
                    hold(pe, (s["att_p"], s["pt0_sb"])[half], n + 1, passed["pe"])
                    for b in ((0, 1), (2,))[half]:
                        col = (b % 2) * 198
                        for k, (a, j) in enumerate(((0, 0), (1, 0), (1, 1))):
                            last = nc.tensor.transpose(Ck[0:HALF, col + k * HALF:col + (k + 1) * HALF],
                                                       probn[:, 2 * b + a, j * HALF:(j + 1) * HALF], ident[0:HALF, 0:HALF])
                    last.then_inc(s[("pt0", "pt1")[half]], 1)
                if slot == 28:
                    hold(pe, s["pt1_sb"], n + 1, passed["pe"])
                    for b in range(NB):
                        nc.tensor.matmul(Ck[0:C, b * T:(b + 1) * T], v_s[:, 2 * b, :], pT[:, b * 198:b * 198 + T], start=True, stop=False)
                        last = nc.tensor.matmul(Ck[0:C, b * T + HALF:(b + 1) * T], v_s[:, 2 * b + 1, :],
                                                pT[:, b * 198 + T:b * 198 + 198], start=False, stop=True)
                    last.then_inc(s["pv"], 1)

            def mix(c):
                last = nc.tensor.matmul(kv_b[:, 0:BLK], tbl[:, c, :], wt[c % 4][:], start=(c == 0), stop=(c == CHUNKS - 1))
                if c % 8 == 7:
                    last.then_inc(s["mixed"], 1)

            side_scores(0)
            for slot in range(32):
                select(0, slot)
            pe.wait_ge(d_tbl[3], 16)
            pe.wait_ge(s["weights"], 1)
            nc.tensor.matmul(kv_b[:, 0:BLK], tbl[:, CHUNKS - AHEAD, :], wt[1][:], start=True, stop=False)
            with pe.Fori(0, HEADS) as h:
                with pe.Fori(0, NBLK // 2) as i:
                    for p in range(2):
                        g = h * NBLK + i * 2 + p
                        for c in range(CHUNKS):
                            if c == 0:
                                pe.wait_ge(s["ranks_sb"], g + 1)
                                pe.wait_ge(d_pairs[p], (h * (NBLK // 2) + i) * 128 + 128)
                            pe.wait_ge(s["weights"], g * CHUNKS + (c + (2 if c < 2 else 1)))
                            q = c // 8
                            nc.tensor.matmul(mask_b[c % 3][:, 0:BLK], sel_mask[:, c, :], ranks[p][:], start=True, stop=True)
                            pe.wait_ge(s["probs"], g * CHUNKS + (c + 1))
                            nc.tensor.matmul(score_b[c % 2][:, 0:BLK], sel_score[:, c % 8, :], pairs[p][:, q // 2, q % 2, :],
                                             start=True, stop=True).then_inc(s["scores"], 1)
                            if c == AHEAD:
                                select(g + 1, c)
                                attend(g, c)
                                pe.wait_ge(s["kv_sb"], g + 1)
                            if c % 8 == AHEAD:
                                pe.wait_ge(d_tbl[c // 8], h * 16 + 16)
                            mix((c - AHEAD) % CHUNKS)
                            if c != AHEAD:
                                select(g + 1, c)
                                attend(g, c)
            pe.wait_ge(s["weights"], STEPS * CHUNKS + AHEAD)
            for c in range(CHUNKS - AHEAD, CHUNKS):
                mix(c)
            pe.wait_ge(s["ranks_sb"], STEPS + 1)
            for g in range(STEPS, STEPS + LAG):
                for slot in range(32):
                    attend(g, slot)

        @block.scalar
        def _(act):
            def copy_scores(n):
                act.wait_ge(s["sims"], n + 1)
                nc.scalar.activation(S[:].rearrange("p t a k -> p (t a k)"), Ck[:, 0:BLK], ACT.Copy).then_inc(s["sims_sb"], 1)

            def select(n, slot):
                if slot == 31:
                    copy_scores(n + 1)
                if slot == 13:
                    act.wait_ge(s["idxs"], n + 1)
                    nc.scalar.activation(idxf[:], idx[:], ACT.Copy).then_inc(s["idxf_sb"], 1)
                if slot == 14:
                    act.wait_ge(s["below"], n + 1)
                    nc.scalar.activation(top_exp[:], below[:], ACT.Exp).then_inc(s["top_exp"], 1)
                if slot == 5:
                    act.wait_ge(s["shifted"], n + 1)
                    nc.scalar.activation(sc_hi[:], sc[:].rearrange("p t a k -> p t (a k)"), ACT.Copy).then_inc(s["hi"], 1)
                if slot in (11, 12):
                    x = slot - 11
                    act.wait_ge(s["turned"], n + 1)
                    if x == 0 and not first(n):
                        act.wait_ge(d_pairs[n_parity[0]], moved[0])
                    last = nc.scalar.activation(split[:, x, :], Bk[:].bitcast(f16)[:, x * BLK:(x + 1) * BLK], ACT.Copy)
                    if x == 1:
                        last.then_inc(s["split_sb"], 1)
                if slot == 21:
                    act.wait_ge(s["rz_ps"], n + 1)
                    if not first(n):
                        act.wait_ge(s["kv_sb"], n)
                    nc.scalar.activation(rz[n_parity[1]][:], Bk[:, 0:BLK], ACT.Copy).then_inc(s["rz_sb"], 1)
                if slot == 30:
                    act.wait_ge(s["ranks_ps"], n + 1)
                    nc.scalar.activation(ranks[n_parity[1]][:], Bk[:, 0:BLK], ACT.Copy).then_inc(s["ranks_sb"], 1)

            n_parity, moved = [1, 0], [None]

            def attend(n, slot):
                if slot == 3:
                    act.wait_ge(s["q_ps"], n + 1)
                    nc.scalar.activation(qT[:], Ck[0:C, 0:ATT], ACT.Copy, scale=C ** -0.5).then_inc(s["q_sb"], 1)
                if slot == 4:
                    act.wait_ge(s["v_ps"], n + 1)
                    nc.scalar.activation(v_s[:].rearrange("p k c -> p (k c)"), Bk[0:HALF, 0:2 * NB * C], ACT.Copy).then_inc(s["v_sb"], 1)
                if 11 <= slot < 17:
                    k = slot - 11
                    if k % 2 == 0:
                        act.wait_ge(s["negmax"], n * NB + (k // 2 + 1))
                    last = nc.scalar.activation(prob[:, k, :], sim[:, k, :], ACT.Exp, bias=negmax[:, k:k + 1], accum_out=psum_[:, k:k + 1])
                    if k == 5:
                        last.then_inc(s["att_exp"], 1)
                if slot == 24:
                    act.wait_ge(s["pt0"], n + 1)
                    nc.scalar.activation(pT[:, 0:396], Ck[0:HALF, 0:396], ACT.Copy).then_inc(s["pt0_sb"], 1)
                if slot == 26:
                    act.wait_ge(s["pt1"], n + 1)
                    nc.scalar.activation(pT[:, 396:594], Ck[0:HALF, 0:198], ACT.Copy).then_inc(s["pt1_sb"], 1)
                if slot == 29:
                    act.wait_ge(s["pv"], n + 1)
                    act.wait_ge(d_o, n * 16 + 16)
                    nc.scalar.activation(oT[:], Ck[0:C, 0:ATT], ACT.Copy).then_inc(s["o_sb"], 1)

            act.sem_inc(s["o_sb"], 1)
            for k in range(2):
                act.sem_inc(s["probs"], 1)
            act.dma_start(oT[:], yT_d[:, 0:ATT]).then_inc(d_o, 16)
            act.dma_start(kv_s[:], kv_d[0][:, 0:BLK]).then_inc(d_kv, 16)
            copy_scores(0)
            for slot in range(32):
                select(0, slot)
            with act.Fori(0, HEADS) as h:
                with act.Fori(0, NBLK // 2) as i:
                    for p in range(2):
                        g = h * NBLK + i * 2 + p
                        n_parity[:] = [p, 1 - p]
                        moved[0] = (h * (NBLK // 2) + i) * 128 + 128
                        for c in range(CHUNKS):
                            act.wait_ge(s["scores"], g * CHUNKS + (c + 1))
                            nc.scalar.activation(ex[c % 4][:], score_b[c % 2][:, 0:BLK], ACT.Exp).then_inc(s["probs"], 1)
                            select(g + 1, c)
                            attend(g, c)
            for g in range(STEPS, STEPS + LAG):
                for slot in range(32):
                    attend(g, slot)

        @block.vector
        def _(dve):
            def select(n, slot):
                if slot in (0, 1):
                    if slot == 0:
                        hold(dve, s["sims_sb"], n + 1, passed["dve"])
                    for t, a in GROUPS[slot]:
                        last = nc.vector.max(val[:, t, a, 0:8], S[:, t, a, :])
                    if slot == 1:
                        last.then_inc(s["firsts"], 1)
                if slot in (2, 3, 4):
                    if slot == 2:
                        dve.drain()
                    for t, a in PARTS[slot - 2]:
                        nc.vector.max_index(idx[:, t, a, 0:8], val[:, t, a, 0:8], S[:, t, a, :])
                        nc.vector.match_replace(S2[:, t, a, :], val[:, t, a, 0:8], S[:, t, a, :], LOWEST)
                if slot in (5, 6):
                    if slot == 5:
                        dve.drain()
                    for t, a in GROUPS[slot - 5]:
                        last = nc.vector.max(val[:, t, a, 8:16], S2[:, t, a, :])
                    if slot == 6:
                        last.then_inc(s["vals"], 1)
                if slot in (7, 8):
                    if slot == 7:
                        dve.drain()
                    for t, a in GROUPS[slot - 7]:
                        last = nc.vector.max_index(idx[:, t, a, 8:16], val[:, t, a, 8:16], S2[:, t, a, :])
                    if slot == 8:
                        last.then_inc(s["idxs"], 1)
                if slot in (9, 11):
                    if slot == 9:
                        hold(dve, s["cands"], n + 1, passed["dve"])
                    else:
                        dve.drain()
                    k = (slot - 9) // 2
                    for t in range(TILES):
                        last = nc.vector.max(best[:, t, 8 * k:8 * k + 8], (cand, cand1)[k][:, t, :])
                    if k == 1:
                        last.then_inc(s["best_v"], 1)
                if slot in (10, 12):
                    dve.drain()
                    k = (slot - 10) // 2
                    for t in range(TILES):
                        nc.vector.match_replace((cand1, cand2)[k][:, t, :], best[:, t, 8 * k:8 * k + 8], (cand, cand1)[k][:, t, :], LOWEST)
                if slot == 13:
                    dve.drain()
                    nc.vector.tensor_tensor(picked[:], cand2[:], cand[:], ALU.not_equal)
                if slot == 14:
                    dve.drain()
                    for a, rows, cols, at in CAND:
                        src = picked[:, :, at:at + rows * cols].rearrange("p t (a b) -> p t a b", a=rows)
                        if cols > 1:
                            with nc.allow_low_precision(reason="counts up to 16"):
                                nc.vector.tensor_reduce(kept[:, :, a:a + rows], src, AX.X, ALU.add)
                        else:
                            nc.vector.tensor_copy(kept[:, :, a:a + rows], picked[:, :, at:at + rows])
                if 15 <= slot < 21:
                    k = slot - 15
                    if k == 0:
                        dve.wait_ge(s["idxf_sb"], n + 1)
                        if not first(n):
                            dve.wait_ge(s["oh_two"], n * TILES)
                    t, a = k % 3, 1 - k // 3
                    ranked = idxf[:, t, a, :].unsqueeze(1).broadcast_to([128, NK, TOP])
                    nc.vector.tensor_tensor(is_key[:, t, a * NK:(a + 1) * NK, :], key_of[:], ranked, ALU.is_equal).then_inc(s["is_key"], 1)
                if slot in (21, 22, 23):
                    t = slot - 21
                    if t == 0:
                        dve.wait_ge(s["is_key"], n * (2 * TILES) + 2 * TILES)
                        if not first(n):
                            dve.wait_ge(s["halved"], n * TILES)
                    weight = kept[:, t, :].unsqueeze(1).broadcast_to([128, NK, TOP])
                    nc.vector.tensor_tensor(onehot[:, t, 0:NK, :], is_key[:, t, 0:NK, :], weight, ALU.mult).then_inc(s["oh_one"], 1)
                if slot in (24, 25, 26):
                    t = slot - 24
                    dve.wait_ge(s["oh_two"], n * TILES + (t + 1))
                    dve.wait_ge(s["oh_one"], n * TILES + (t + 1))
                    nc.vector.tensor_tensor(oh_half[:, t], onehot[:, t, :, 0:8], onehot[:, t, :, 8:16], ALU.add).then_inc(s["halved"], 1)
                if slot in (25, 26, 27):
                    t = slot - 25
                    if t == 0 and not first(n):
                        dve.wait_ge(s["ranks_ps"], n)
                    dve.wait_ge(s["halved"], n * TILES + (t + 1))
                    nc.vector.tensor_tensor(oh_quarter[:, t], oh_half[:, t, :, 0:4], oh_half[:, t, :, 4:8], ALU.add).then_inc(s["quartered"], 1)
                if slot == 16:
                    dve.wait_ge(s["top_exp"], n + 1)
                    nc.vector.tensor_reduce(total[:], top_exp[:], AX.X, ALU.add)
                if slot == 17:
                    dve.drain()
                    nc.vector.reciprocal(rtotal[:], total[:]).then_inc(s["rtotal"], 1)

            def scale_kv(n, p):
                dve.wait_ge(s["rz_sb"], n + 1)
                dve.wait_ge(s["mixed"], n * 4 + 1)
                dve.wait_ge(d_kv, n * 16 + 16)
                nc.vector.tensor_tensor(kv_s[:], kv_b[:, 0:BLK], rz[p][:], ALU.mult).then_inc(s["kv_sb"], 1)

            GROUPS = [[(0, 0), (0, 1), (1, 0)], [(1, 1), (2, 0), (2, 1)]]
            PARTS = [[(0, 0), (0, 1)], [(1, 0), (1, 1)], [(2, 0), (2, 1)]]

            def attend(n, slot):
                if slot in (6, 7, 9):
                    b = (6, 7, 9).index(slot)
                    dve.wait_ge(s_sim[b], n + 1)
                    src = (Ck, Bk, Ck)[b]
                    nc.vector.tensor_tensor(sim[:, 2 * b:2 * b + 2, :].rearrange("p a t -> p (a t)"), src[0:HALF, 0:2 * T],
                                            causal[:].rearrange("p a t -> p (a t)"), ALU.add).then_inc(s_msk[b], 1)
                if slot in (7, 8, 10):
                    b = (7, 8, 10).index(slot)
                    dve.wait_ge(s_msk[b], n + 1)
                    nc.vector.tensor_reduce(negmax[:, 2 * b:2 * b + 2], sim[:, 2 * b:2 * b + 2, :], AX.X, ALU.max, negate=True).then_inc(s["negmax"], 1)
                if slot == 16:
                    dve.wait_ge(s["att_exp"], n + 1)
                    nc.vector.reciprocal(prec[:], psum_[:]).then_inc(s["att_rec"], 1)

            nc.vector.memset(rz[1][:], 0.0).then_inc(s["rz_sb"], 1)
            for k in range(1, AHEAD + 1):
                nc.vector.memset(wt[k][:], 0.0).then_inc(s["weights"], 1)
            for slot in range(32):
                select(0, slot)
            with dve.Fori(0, HEADS) as h:
                with dve.Fori(0, NBLK // 2) as i:
                    for p in range(2):
                        g = h * NBLK + i * 2 + p
                        for c in range(CHUNKS):
                            dve.wait_ge(s["probs"], g * CHUNKS + (c + 3))
                            nc.vector.scalar_tensor_tensor(out=wt[c % 4][:], in0=mask_b[c % 3][:, 0:BLK], scalar=float(TOP), in1=ex[c % 4][:],
                                                           op0=ALU.is_gt, op1=ALU.mult).then_inc(s["weights"], 1)
                            if c == AHEAD - 1:
                                scale_kv(g, 1 - p)
                            select(g + 1, c)
                            attend(g, c)
            scale_kv(STEPS, 1)
            for g in range(STEPS, STEPS + LAG):
                for slot in range(32):
                    attend(g, slot)

        @block.gpsimd
        def _(pool):
            def select(n, slot):
                if slot == 7:
                    pool.wait_ge(s["vals"], n + 1)
                    for a, rows, cols, at in CAND:
                        out = cand[:, :, at:at + rows * cols].rearrange("p t (a b) -> p t a b", a=rows)
                        one = val[:, :, 0, a:a + rows].unsqueeze(3).broadcast_to([128, TILES, rows, cols])
                        two = val[:, :, 1, 0:cols].unsqueeze(2).broadcast_to([128, TILES, rows, cols])
                        last = pool.tensor_tensor(out, one, two, ALU.add)
                    last.then_inc(s["cands"], 1)
                if slot == 2:
                    pool.wait_ge(s["firsts"], n + 1)
                    pool.tensor_tensor(sc0[:], S[:], val[:, :, :, 0:1].broadcast_to([128, TILES, 2, NK]), ALU.subtract)
                    pool.drain()
                    pool.tensor_scalar(sc[:], sc0[:], FLOOR, None, ALU.max).then_inc(s["shifted"], 1)
                if slot == 6:
                    pool.wait_ge(s["hi"], n + 1)
                    pool.tensor_tensor(sc_lo[:], sc[:].rearrange("p t a k -> p t (a k)"), sc_hi[:], ALU.subtract).then_inc(s["lo"], 1)
                if slot == 12:
                    pool.wait_ge(s["best_v"], n + 1)
                    pool.tensor_tensor(below[:], best[:], best[:, :, 0:1].broadcast_to([128, TILES, TOP]), ALU.subtract).then_inc(s["below"], 1)
                if slot in (15, 16, 17):
                    t = slot - 15
                    pool.wait_ge(s["is_key"], n * (2 * TILES) + (t + 1))
                    if t == 0 and not first(n):
                        pool.wait_ge(s["halved"], n * TILES)
                    weight = from_top[:].unsqueeze(1).broadcast_to([128, NK, TOP])
                    pool.tensor_tensor(onehot[:, t, NK:, :], is_key[:, t, NK:, :], weight, ALU.mult).then_inc(s["oh_two"], 1)

            def attend(n, slot):
                if slot == 16:
                    pool.wait_ge(s["att_rec"], n + 1)
                    pool.tensor_tensor(probn[:], prob[:], prec[:].unsqueeze(2).broadcast_to([HALF, 2 * NB, T]), ALU.mult).then_inc(s["att_p"], 1)

            for slot in range(32):
                select(0, slot)
            with pool.Fori(0, STEPS) as g:
                for slot in range(32):
                    select(g + 1, slot)
                    attend(g, slot)
            for g in range(STEPS, STEPS + LAG):
                for slot in range(32):
                    attend(g, slot)


def final(nc, ctx, sb, sem, bank, env):
    f32 = env["f32"]
    ALU = env["ALU"]
    h1_d, o_d, wo, out = env["h1_d"], env["o_d"], env["wo"], env["out"]
    passed = env["passed"]
    with ExitStack() as local:
        def sb(name, shape, dt=f32):
            return local.enter_context(nc.sbuf_tensor(name, shape, dt))

        wo_s = sb("wo_s", [128, 4, C])
        ob = [sb(f"ob{p}", [128, 4, BLK]) for p in range(2)]
        hb = [sb(f"hb{p}", [128, TILES, C]) for p in range(2)]
        res = [sb(f"res{p}", [128, TILES, C]) for p in range(2)]
        f_wo, f_mm, f_res = sem("f_wo"), sem("f_mm"), sem("f_res")
        f_in = [sem(f"f_in{p}") for p in range(2)]
        f_out = [sem(f"f_out{p}") for p in range(2)]
        o_v = o_d[1:HEADS + 1].rearrange("(k e) c t -> (e c) k t", e=2)
        h_v = h1_d.rearrange("(n k p) c -> p n k c", k=TILES, p=128)
        out_v = out.rearrange("b t c -> (b t) c").rearrange("(n k p) c -> p n k c", k=TILES, p=128)
        block = local.enter_context(nc.Block())

        @block.sync
        def _(sp):
            def load(n, p):
                sp.dma_start(ob[p][:], o_v[:, :, bass.ds(n * BLK, BLK)]).then_inc(f_in[p], 16)
                sp.dma_start(hb[p][:], h_v[:, bass.ds(n, 1)].rearrange("p o k c -> p (o k) c")).then_inc(f_in[p], 16)

            def store(n, p):
                sp.dma_start(out_v[:, bass.ds(n, 1)].rearrange("p o k c -> p (o k) c"), res[p][:]).then_inc(f_out[p], 16)

            sp.dma_start(wo_s[:], wo.rearrange("(k p) c -> p k c", p=128)).then_inc(f_wo, 16)
            load(0, 0)
            load(1, 1)
            with sp.Fori(0, NBLK // 2 - 1) as i:
                for p in range(2):
                    sp.wait_ge(f_res, i * 2 + (p + 1))
                    store(i * 2 + p, p)
                    load(i * 2 + (p + 2), p)
            for p in range(2):
                sp.wait_ge(f_res, NBLK - 1 + p)
                store(NBLK - 2 + p, p)
            for p in range(2):
                sp.wait_ge(f_out[p], 16 * (NBLK // 2))

        @block.tensor
        def _(pe):
            pe.wait_ge(f_wo, 16)

            def block_of(n, i, p):
                pe.wait_ge(f_in[p], i * 32 + 32)
                if n is not None:
                    pe.wait_ge(f_res, n)
                for t in range(TILES):
                    for k in range(4):
                        last = nc.tensor.matmul(bank[p][:, t * C:(t + 1) * C], ob[p][:, k, t * 128:(t + 1) * 128],
                                                wo_s[:, k, :], start=(k == 0), stop=(k == 3))
                last.then_inc(f_mm, 1)

            for p in range(2):
                block_of(None, 0, p)
            with pe.Fori(1, NBLK // 2) as i:
                for p in range(2):
                    block_of(i * 2 + (p - 1), i, p)

        @block.vector
        def _(dve):
            def block_of(i, p, again):
                dve.wait_ge(f_mm, i * 2 + (p + 1))
                if again:
                    dve.wait_ge(f_out[p], i * 16)
                nc.vector.tensor_tensor(res[p][:].rearrange("p k c -> p (k c)"), bank[p][:, 0:TILES * C],
                                        hb[p][:].rearrange("p k c -> p (k c)"), ALU.add).then_inc(f_res, 1)

            for p in range(2):
                block_of(0, p, False)
            with dve.Fori(1, NBLK // 2) as i:
                for p in range(2):
                    block_of(i, p, True)


_OUTS = [((B, T, C), "float32")]


def kernel(x, txt, L0_tok_weight, L0_tok_bias, L0_attn_time_w, L0_attn_time_mix_k, L0_attn_time_mix_v,
           L0_attn_time_mix_r, L0_attn_Wk, L0_attn_Wv, L0_attn_Wr, L0_attn_Wo, L0_ffn_Wq_pk, L0_ffn_pk_keys,
           L0_ffn_Wq, L0_ffn_keys_table, L0_ffn_values_table, L0_ffn_Wo):
    import numpy as _np
    import concourse.bacc as _bacc
    from concourse import mybir as _mybir
    from concourse.bass_utils import run_bass_kernel_spmd as _run

    a = _np.asarray
    late = a(L0_attn_time_w)[::-1]
    distance = _np.abs(_np.arange(T)[None, :] - _np.arange(T)[:, None])
    mix = _np.stack([a(m).reshape(C) for m in (L0_attn_time_mix_k, L0_attn_time_mix_v, L0_attn_time_mix_r)], axis=1)
    wkvr = _np.concatenate([a(L0_attn_Wk), a(L0_attn_Wv), a(L0_attn_Wr)], axis=1)

    def rows(tab):
        return a(tab).reshape(HEADS, 2, 32, 2, 8, 4, C).transpose(0, 5, 2, 3, 1, 4, 6).reshape(HEADS, 128, CHUNKS, C)

    wq = a(L0_ffn_Wq).reshape(C, HEADS, C).transpose(1, 0, 2)
    ins = {
        "x": a(x), "txt": a(txt), "tok_w": a(L0_tok_weight), "tok_b": a(L0_tok_bias),
        "toeplitz": late[distance],
        "mix": _np.concatenate([mix, mix], axis=0), "wkvr": _np.concatenate([wkvr, wkvr], axis=0),
        "attn_wo": a(L0_attn_Wo),
        "wqT": a(L0_ffn_Wq_pk).reshape(C, 2, HEADS, DK).transpose(3, 2, 1, 0).reshape(DK, 2 * HEADS, C),
        "keysT": a(L0_ffn_pk_keys).transpose(3, 2, 0, 1).reshape(DK, 2 * HEADS, NK),
        "wq": _np.concatenate([wq[:1], wq], axis=0),
        "table": _np.concatenate([rows(L0_ffn_keys_table), rows(L0_ffn_values_table)], axis=3),
        "wo": a(L0_ffn_Wo),
    }
    nc = _bacc.Bacc("TRN2", target_bir_lowering=False, num_devices=1)
    arrays, args = {}, []
    for name, v in ins.items():
        v = _np.ascontiguousarray(v)
        arrays[f"in_{name}"] = v
        args.append(nc.dram_tensor(f"in_{name}", v.shape, _mybir.dt.from_np(v.dtype), kind="ExternalInput").ap())
    shape, dtype = _OUTS[0]
    args.append(nc.dram_tensor("out_0", shape, _mybir.dt.from_np(_np.dtype(dtype)), kind="ExternalOutput").ap())
    build(nc, *args)
    r = _run(nc, [arrays], core_ids=[0])
    return r.results[0]["out_0"]
```
